# Optimizing a Trainium2 kernel written in Bass

```python
import numpy as np
import jax
import jax.numpy as jnp

def _softmax(x, axis=-1):
    return jax.nn.softmax(x, axis=axis)

def _gelu(x):
    return jax.nn.gelu(x, approximate=True)

def _silu(x):
    return jax.nn.silu(x)

def _sigmoid(x):
    return jax.nn.sigmoid(x)

def _layernorm(x, axis=-1, eps=1e-05):
    m = jnp.mean(x, axis=axis, keepdims=True)
    v = jnp.var(x, axis=axis, keepdims=True)
    return (x - m) / jnp.sqrt(v + eps)

def _scatter_add(tgt, idx, src, axis=0):
    return tgt.at[idx].add(src)

def _segment_sum(src, seg, n):
    return jax.ops.segment_sum(src, seg, n)
kernel_name = 'mk_perceiver_d1_seqx_r2_31ae89'

def setup_inputs(seed: int=0):
    np.random.seed(seed)
    _w = jnp.asarray

    def _rec_inputs():
        import jax
        import jax.numpy as jnp
        _rk = jax.random.key(seed)
        x = -0.0003929 + 0.9999 * jax.random.normal(jax.random.fold_in(_rk, 1), (16, 128, 512), jnp.float32)
        _lenS = 128 - jax.random.randint(jax.random.fold_in(_rk, 7), (16,), 0, max(1, 128 // 4) + 1, jnp.int32)
        _lenS2 = 2048 - jax.random.randint(jax.random.fold_in(_rk, 8), (16,), 0, max(1, 2048 // 4) + 1, jnp.int32)
        _ctx_1024P = jax.random.normal(jax.random.fold_in(_rk, 11), (16, 16, 512), jnp.float32)
        _ctx_1024c = jax.random.dirichlet(jax.random.fold_in(_rk, 511), 0.3 * jnp.ones((16,), jnp.float32), (16, 2048))
        _ctx_1024t = jnp.einsum('bsk,bkd->bsd', _ctx_1024c, _ctx_1024P)
        _ctx_1024t = _ctx_1024t * jax.lax.rsqrt(jnp.mean(jnp.square(_ctx_1024t)) + 1e-12) * 0.953939
        ctx_1024 = 4.13588e-05 + 0.999923 * (_ctx_1024t + 0.3 * jax.random.normal(jax.random.fold_in(_rk, 611), (16, 2048, 512), jnp.float32))
        return (x, ctx_1024)
    x, ctx_1024 = _rec_inputs()

    def _L0_xattn_setup():
        import jax, jax.numpy as jnp
        import numpy as np
        key = jax.random.key(seed)
        k1, k2 = jax.random.split(key)
        B, L, V, D = (8, 1024, 512, 512)
        hidden_states = jax.random.normal(k1, (B, L, D), dtype=jnp.float32)
        visual_hidden_state = jax.random.normal(k2, (B, V, D), dtype=jnp.float32)
        return {'hidden_states': hidden_states, 'visual_hidden_state': visual_hidden_state}
    _L0_xattn_all = _L0_xattn_setup()
    _L0_xattn_in = {k: v for k, v in _L0_xattn_all.items() if k in ()}
    del _L0_xattn_all

    def _L0_attn_setup():
        import jax, jax.numpy as jnp
        import numpy as np
        import math
        B, T, C = (2, 1024, 512)
        H, L = (16, 64)
        DH = C // H
        DHE = DH // 2
        THETA = 10000.0

        def _rope_cache(t, dim):
            inv_freq = 1.0 / THETA ** (jnp.arange(0, dim, 2, dtype=jnp.float32) / dim)
            freqs = jnp.arange(t, dtype=jnp.float32)[:, None] * inv_freq[None, :]
            emb = jnp.concatenate((freqs, freqs), axis=-1)
            return (jnp.cos(emb), jnp.sin(emb))

        def _apply_rope(x, cos, sin):
            x1 = x[..., 0::2]
            x2 = x[..., 1::2]
            rot = jnp.stack((-x2, x1), axis=-1).reshape(x.shape)
            return x * cos[None, None] + rot * sin[None, None]
        key = jax.random.key(seed)
        ks = jax.random.split(key, 10)
        s = 0.02
        return {'x': jax.random.normal(ks[0], (B, T, C), jnp.float32), 'Wq_down': jax.random.normal(ks[1], (C, H * L), jnp.float32) * s, 'Wk_down': jax.random.normal(ks[2], (C, H * L), jnp.float32) * s, 'Wv_down': jax.random.normal(ks[3], (C, H * L), jnp.float32) * s, 'Wq_up_c': jax.random.normal(ks[4], (L, DHE), jnp.float32) * s, 'Wq_up_e': jax.random.normal(ks[5], (L, DHE), jnp.float32) * s, 'Wk_up_c': jax.random.normal(ks[6], (L, DHE), jnp.float32) * s, 'Wk_up_e': jax.random.normal(ks[7], (L, DHE), jnp.float32) * s, 'Wv_up': jax.random.normal(ks[8], (L, DH), jnp.float32) * s, 'Wc': jax.random.normal(ks[9], (C, C), jnp.float32) * s}
    _L0_attn_all = _L0_attn_setup()
    _L0_attn_in = {k: v for k, v in _L0_attn_all.items() if k in ('Wq_down', 'Wk_down', 'Wv_down', 'Wq_up_c', 'Wq_up_e', 'Wk_up_c', 'Wk_up_e', 'Wv_up', 'Wc')}
    del _L0_attn_all

    def _L0_ffn_setup():
        import jax, jax.numpy as jnp
        import numpy as np
        B, L, H = (8, 1024, 512)
        E, K, R = (8, 2, 64)

        def _gates(cls_tok, Wr):
            logits = cls_tok @ Wr.T
            top_vals, top_idx = jax.lax.top_k(logits, K)
            neg_inf = jnp.full_like(logits, -jnp.inf)
            rows = jnp.arange(logits.shape[0])[:, None]
            masked = neg_inf.at[rows, top_idx].set(top_vals)
            return jax.nn.softmax(masked, axis=-1)
        key = jax.random.key(seed)
        k1, k2, k3, k4 = jax.random.split(key, 4)
        x = jax.random.normal(k1, (B, L, H), dtype=jnp.float32)
        Wr = jax.random.normal(k2, (E, H), dtype=jnp.float32) * (1.0 / np.sqrt(H))
        A = jax.random.normal(k3, (E, R, H), dtype=jnp.float32) * (1.0 / np.sqrt(H))
        Bw = jax.random.normal(k4, (E, H, R), dtype=jnp.float32) * (1.0 / np.sqrt(R))
        return {'x': x, 'Wr': Wr, 'A': A, 'Bw': Bw}
    _L0_ffn_all = _L0_ffn_setup()
    _L0_ffn_in = {k: v for k, v in _L0_ffn_all.items() if k in ('Wr', 'A', 'Bw')}
    del _L0_ffn_all
    return {'x': x, 'ctx_1024': ctx_1024, 'L0_attn_Wq_down': _L0_attn_in['Wq_down'], 'L0_attn_Wk_down': _L0_attn_in['Wk_down'], 'L0_attn_Wv_down': _L0_attn_in['Wv_down'], 'L0_attn_Wq_up_c': _L0_attn_in['Wq_up_c'], 'L0_attn_Wq_up_e': _L0_attn_in['Wq_up_e'], 'L0_attn_Wk_up_c': _L0_attn_in['Wk_up_c'], 'L0_attn_Wk_up_e': _L0_attn_in['Wk_up_e'], 'L0_attn_Wv_up': _L0_attn_in['Wv_up'], 'L0_attn_Wc': _L0_attn_in['Wc'], 'L0_ffn_Wr': _L0_ffn_in['Wr'], 'L0_ffn_A': _L0_ffn_in['A'], 'L0_ffn_Bw': _L0_ffn_in['Bw']}

def reference(x, ctx_1024, L0_attn_Wq_down, L0_attn_Wk_down, L0_attn_Wv_down, L0_attn_Wq_up_c, L0_attn_Wq_up_e, L0_attn_Wk_up_c, L0_attn_Wk_up_e, L0_attn_Wv_up, L0_attn_Wc, L0_ffn_Wr, L0_ffn_A, L0_ffn_Bw):
    import jax
    import jax.numpy as jnp

    def _L0_xattn_ref(hidden_states, visual_hidden_state):
        import jax, jax.numpy as jnp
        import numpy as np
        scores = jnp.einsum('bld,bvd->blv', hidden_states, visual_hidden_state)
        probs = jax.nn.softmax(scores, axis=-1)
        return jnp.einsum('blv,bvd->bld', probs, visual_hidden_state)

    def _L0_attn_ref(x, Wq_down, Wk_down, Wv_down, Wq_up_c, Wq_up_e, Wk_up_c, Wk_up_e, Wv_up, Wc):
        import jax, jax.numpy as jnp
        import numpy as np
        import math
        B, T, C = (2, 1024, 512)
        H, L = (16, 64)
        DH = C // H
        DHE = DH // 2
        THETA = 10000.0

        def _rope_cache(t, dim):
            inv_freq = 1.0 / THETA ** (jnp.arange(0, dim, 2, dtype=jnp.float32) / dim)
            freqs = jnp.arange(t, dtype=jnp.float32)[:, None] * inv_freq[None, :]
            emb = jnp.concatenate((freqs, freqs), axis=-1)
            return (jnp.cos(emb), jnp.sin(emb))

        def _apply_rope(x, cos, sin):
            x1 = x[..., 0::2]
            x2 = x[..., 1::2]
            rot = jnp.stack((-x2, x1), axis=-1).reshape(x.shape)
            return x * cos[None, None] + rot * sin[None, None]
        b, t, c = x.shape
        q_lat = (x @ Wq_down).reshape(b, t, H, L)
        k_lat = (x @ Wk_down).reshape(b, t, H, L)
        v_lat = (x @ Wv_down).reshape(b, t, H, L)
        q_c = jnp.einsum('bthl,ld->bhtd', q_lat, Wq_up_c)
        q_e = jnp.einsum('bthl,ld->bhtd', q_lat, Wq_up_e)
        k_c = jnp.einsum('bthl,ld->bhtd', k_lat, Wk_up_c)
        k_e = jnp.einsum('bthl,ld->bhtd', k_lat, Wk_up_e)
        v = jnp.einsum('bthl,ld->bhtd', v_lat, Wv_up)
        cos, sin = _rope_cache(t, DHE)
        q = jnp.concatenate([q_c, _apply_rope(q_e, cos, sin)], axis=-1)
        k = jnp.concatenate([k_c, _apply_rope(k_e, cos, sin)], axis=-1)
        scale = 1.0 / math.sqrt(DH)
        scores = jnp.einsum('bhqd,bhkd->bhqk', q, k) * scale
        causal = jnp.tril(jnp.ones((t, t), dtype=bool))
        scores = jnp.where(causal[None, None], scores, -jnp.inf)
        att = jax.nn.softmax(scores, axis=-1)
        y = jnp.einsum('bhqk,bhkd->bhqd', att, v)
        y = y.transpose(0, 2, 1, 3).reshape(b, t, c)
        return y @ Wc

    def _L0_ffn_ref(x, Wr, A, Bw):
        import jax, jax.numpy as jnp
        import numpy as np
        B, L, H = (8, 1024, 512)
        E, K, R = (8, 2, 64)

        def _gates(cls_tok, Wr):
            logits = cls_tok @ Wr.T
            top_vals, top_idx = jax.lax.top_k(logits, K)
            neg_inf = jnp.full_like(logits, -jnp.inf)
            rows = jnp.arange(logits.shape[0])[:, None]
            masked = neg_inf.at[rows, top_idx].set(top_vals)
            return jax.nn.softmax(masked, axis=-1)
        gates = _gates(x[:, 0, :], Wr)
        mid = jnp.einsum('blh,erh->belr', x, A)
        expert_out = jnp.einsum('belr,ehr->belh', mid, Bw)
        weighted = jnp.einsum('be,belh->blh', gates, expert_out)
        return x + weighted
    x = x + _L0_xattn_ref(_layernorm(x, axis=-1), ctx_1024)
    x = x + _L0_attn_ref(_layernorm(x, axis=-1), L0_attn_Wq_down, L0_attn_Wk_down, L0_attn_Wv_down, L0_attn_Wq_up_c, L0_attn_Wq_up_e, L0_attn_Wk_up_c, L0_attn_Wk_up_e, L0_attn_Wv_up, L0_attn_Wc)
    x = x + _L0_ffn_ref(_layernorm(x, axis=-1), L0_ffn_Wr, L0_ffn_A, L0_ffn_Bw)
    return x

_drawn_inputs = setup_inputs


def setup_inputs(seed=0):
    import zlib

    import numpy as np

    out = dict(_drawn_inputs(seed))
    spreads = {}
    factors = {'L0_attn_Wq_down': 8.0,
     'L0_attn_Wk_down': 8.0,
     'L0_attn_Wv_down': 8.0,
     'L0_attn_Wq_up_c': 8.0,
     'L0_attn_Wq_up_e': 8.0,
     'L0_attn_Wk_up_c': 8.0,
     'L0_attn_Wk_up_e': 8.0,
     'L0_attn_Wc': 8.0}
    for name, (base, spread) in spreads.items():
        noise = np.random.default_rng([zlib.crc32(name.encode()), seed]).standard_normal(out[name].shape)
        drawn = base * np.exp(spread * noise) if base else spread * noise
        out[name] = jnp.asarray(drawn.astype(out[name].dtype))
    for name, factor in factors.items():
        out[name] = (out[name] * factor).astype(out[name].dtype)
    return out
```

```python
import numpy as np
import concourse.bass as bass
from concourse import mybir
from contextlib import ExitStack

F32, F32R, BF16, U32 = mybir.dt.float32, mybir.dt.float32r, mybir.dt.bfloat16, mybir.dt.uint32
ALU, ACT, AX = mybir.AluOpType, mybir.ActivationFunctionType, mybir.AxisListType

P = 128
NB, T, D, S = 16, 128, 512, 2048
H, L, DH = 16, 64, 32
DHE = DH // 2
E, R = 8, 64
KD = D // P
NCH = S // 512
HG = H // 4
PIECE = 1024
NPT = 8
RAW, SPLIT = 6, 5
VW = 3 * DH + 1
EPS = 1e-5
MASK = -1e30


class Lane:

    def __init__(self, sem, step=1):
        self.sem, self.step, self.count, self.queue, self.waited = sem, step, 0, [], {}

    def do(self, make, *after, signal=True):
        waits = []
        for lane, value in filter(None, after):
            if self.waited.get(lane, 0) < value:
                self.waited[lane] = value
                waits.append((lane.sem, value))
        self.queue.append((waits, make, signal))
        self.count += signal
        return (self, self.count) if signal else None

    def play(self, eng):
        for waits, make, signal in self.queue:
            for sem, value in waits:
                eng.wait_ge(sem, value)
            made = make(eng)
            if signal:
                made.then_inc(self.sem, 1)


class Loads:

    def __init__(self, sem):
        self.sem, self.count = sem, 0

    def load(self, lane, make, *after):
        self.count += 16
        sem = self.sem
        lane.do(lambda e: make(e).then_inc(sem, 16), *after, signal=False)
        return (self, self.count)


def perceiver(nc, x, ctxT, ctx, wdT, wup_c, wup_e, wup_v, wc, wrT, expA, expB, cos_t, sin_t, mask_t, ident_t,
              slot_t, out):
    with ExitStack() as stack:
        def sb(name, shape, dt=F32):
            return stack.enter_context(nc.sbuf_tensor(name, shape, dt))

        def ps(name, shape, dt=F32):
            return stack.enter_context(nc.psum_tensor(name, shape, dt))

        def sem(name):
            return stack.enter_context(nc.semaphore(name))

        raw = sb("ctx_raw", [P, RAW, PIECE])
        hi = sb("ctx_high", [P, SPLIT, PIECE], F32R)
        lo = sb("ctx_low", [P, SPLIT, PIECE], F32R)
        prob = sb("cross_prob", [P, S])
        pT_hi = sb("cross_probT_high", [P, 2, 512], F32R)
        pT_lo = sb("cross_probT_low", [P, 2, 512], F32R)
        w_hi = sb("wqkv_high", [P, KD, 3 * D], F32R)
        w_lo = sb("wqkv_low", [P, KD, 3 * D], F32R)
        wc_hi = sb("wc_high", [P, KD, D], F32R)
        wc_lo = sb("wc_low", [P, KD, D], F32R)
        x_in = sb("x_in", [P, 2, D])
        x1 = sb("x1", [P, D])
        xn = sb("x_normed", [P, D])
        xn1 = sb("x_normed_first", [P, D])
        q1_hi = sb("cross_qT_high", [P, 2, D], F32R)
        q1_lo = sb("cross_qT_low", [P, 2, D], F32R)
        t_hi = sb("tokensT_high", [P, D], F32R)
        t_lo = sb("tokensT_low", [P, D], F32R)
        qk = sb("qk_roped", [P, 2, D])
        rope_b = sb("rope_scratch", [P, 2 * H, DHE])
        qT = sb("qT", [P, D])
        kbd = sb("kT_block_diagonal", [P, HG, 512])
        vp = sb("v_parts", [P, H, VW], BF16)
        v_res = sb("v_residue", [P, D])
        sc = sb("self_scores", [P, 2, 512])
        p_part = sb("self_probT_parts", [P, 2, 3, 512], BF16)
        p_res = sb("self_probT_residue", [P, 512])
        y = sb("y", [P, D])
        ya = sb("expert_A", [P, KD, 2 * R])
        yb = sb("expert_B", [P, D])
        midT = sb("midT", [P, T])
        wr = sb("wrT", [P, KD, E])
        cosb = sb("rope_cos", [P, DHE])
        sinb = sb("sin_signed", [P, DHE])
        mask = sb("causal_mask", [P, T])
        ident = sb("identity", [P, P])
        slot = sb("second_expert", [P, 2])
        powm = sb("minus_half", [P, 1])
        st = sb("stats", [P, 3, 16])
        cmax = sb("cross_chunk_max", [P, NCH])
        nmax = sb("cross_neg_max", [P, 1])
        rsum = sb("cross_row_sums", [P, NCH])
        rinv = sb("cross_row_inverse", [P, 2])
        smax = sb("self_max", [P, 2, 4])
        sinv = sb("self_sum_inverse", [P, 4])
        top = sb("gate_top", [P, 8])
        topi = sb("gate_index", [P, 8], U32)
        gt = sb("gate_scratch", [P, 8])

        bank_s = [ps(f"bank_scores{i}", [P, 512]) for i in range(2)]
        bank_t = [ps(f"bank_transposed{i}", [P, 512]) for i in range(2)]
        bank_o = ps("bank_cross_out", [P, 512])
        bank_a = ps("banks_self", [P, 3, 512])

        pe, act, dve, pool, sp = (Lane(sem(n)) for n in ("pe", "act", "dve", "pool", "sp"))
        setup_loads = Loads(sem("setup_loads"))
        down_loads = [Loads(sem(f"down_loads{j}")) for j in range(3)]
        piece_loads = [Loads(sem(f"piece_loads{i}")) for i in range(RAW)]
        x_loads = [Loads(sem(f"x_loads{i}")) for i in range(2)]
        expert_loads = Loads(sem("expert_loads"))
        stores = Loads(sem("stores"))

        def f32(ap):
            return ap.bitcast(F32)

        def hi_lo(src, high, low, *after):
            e_hi = act.do(lambda e: e.activation(high, src, ACT.Copy), *after)
            return dve.do(lambda e: e.tensor_tensor(low, src, f32(high), ALU.subtract), e_hi, *after)

        def mm(o, a, b, start, stop, *after, signal=False, **kw):
            return pe.do(lambda e: e.matmul(o, a, b, start=start, stop=stop, **kw), *after, signal=signal)

        def transpose4(bank, tiles, *after):
            for i, tile in enumerate(tiles):
                ev = pe.do(lambda e, i=i, tile=tile: e.transpose(bank[:, i * P:(i + 1) * P], tile, ident[:, :]),
                           *after, signal=i == 3)
            return ev

        class Ring:

            def __init__(self, bufs):
                self.bufs, self.free, self.n = bufs, [None] * len(bufs), -1

            def take(self):
                self.n += 1
                self.i = self.n % len(self.bufs)
                return self.i, self.bufs[self.i], self.free[self.i]

        ring_t = Ring([b[:, :] for b in bank_t])
        ring_s = Ring([b[:, :] for b in bank_s])
        ring_a = Ring([bank_a[:, i, :] for i in range(3)])
        ring_p = Ring([0, 1])
        ring_sc = Ring([0, 1])
        ring_pp = Ring([0, 1])

        def load(dst, src, *after):
            return setup_loads.load(sp, lambda e: e.dma_start(dst, src), *after)

        stage = prob[:, :].rearrange("p (k n) -> p k n", k=KD)
        up = sc[:, 0, 0:192].rearrange("p (j n) -> p j n", j=3)
        z_up = dve.do(lambda e: e.memset(sc[:, :, :], 0.0))
        z_kbd = dve.do(lambda e: e.memset(kbd[:, :, :], 0.0))
        c_pow = dve.do(lambda e: e.memset(powm[:, :], -0.5))
        one_vp = dve.do(lambda e: e.memset(vp[:, :, 3 * DH:VW], 1.0))
        load(ident[:, :], ident_t)
        load(x_in[:, 0, :], x[0])
        load(cosb[:, :], cos_t)
        load(sinb[:, :], sin_t)
        load(mask[:, :], mask_t)
        load(slot[:, :], slot_t)
        load(wr[:, :, :], wrT)
        for g in range(2):
            rows = slice(g * L, (g + 1) * L)
            for j in range(2):
                load(up[rows, j, g * DH:g * DH + DHE], wup_c[j], z_up)
                load(up[rows, j, g * DH + DHE:(g + 1) * DH], wup_e[j])
            load(up[rows, 2, g * DH:(g + 1) * DH], wup_v)
        consts = load(stage, wc.rearrange("(k p) n -> p k n", p=P))
        wc_split = hi_lo(stage, wc_hi[:, :, :], wc_lo[:, :, :], consts)

        pieces = {}
        sent = [0]
        raw_free, split_free = [None] * RAW, [None] * SPLIT

        def send_piece():
            n = sent[0]
            if n >= NB * 2 * NPT:
                return
            sent[0] += 1
            b, i = divmod(n, 2 * NPT)
            src = ctxT[b, i] if i < NPT else ctx[b, i - NPT]
            r = n % RAW
            pieces[n] = piece_loads[r].load(sp, lambda e: e.dma_start(raw[:, r, :], src), raw_free[r])

        def split_piece(n):
            r, s = n % RAW, n % SPLIT
            natural = n % (2 * NPT) >= NPT
            e_hi = act.do(lambda e: e.activation(hi[:, s, :], raw[:, r, :], ACT.Copy), pieces[n], split_free[s])
            lane = pool if natural else dve
            e_lo = lane.do(lambda e: e.tensor_tensor(lo[:, s, :], raw[:, r, :], f32(hi[:, s, :]), ALU.subtract),
                           pieces[n], split_free[s], e_hi)
            raw_free[r] = e_lo
            send_piece()
            split_done[n] = (e_hi, e_lo)

        split_done = {}
        split_next = [0]

        def split_ahead(upto):
            while split_next[0] < min(upto, NB * 2 * NPT):
                split_piece(split_next[0])
                split_next[0] += 1

        def next_piece(use):
            assert use < split_next[0]
            return use % SPLIT, split_done[use]

        stat_free = [None] * 3

        def layernorm(which, src, dst, ready, *dst_free):
            s = st[:, which, :]
            a = dve.do(lambda e: e.bn_stats(s[:, 0:6], src), ready, stat_free[which])
            a = dve.do(lambda e: e.bn_aggr(s[:, 8:10], s[:, 0:6]), a)
            a = dve.do(lambda e: e.tensor_scalar(s[:, 10:11], s[:, 9:10], EPS, None, ALU.add), a)
            a = pool.do(lambda e: e.tensor_tensor(s[:, 11:12], s[:, 10:11], powm[:, :], ALU.pow), a, c_pow)
            a = dve.do(lambda e: e.tensor_scalar(dst, src, s[:, 8:9], s[:, 11:12], ALU.subtract, ALU.mult), a, *dst_free)
            stat_free[which] = a
            return a

        def chunks(t):
            return [t[:, c * P:(c + 1) * P] for c in range(KD)]

        x_ready = {0: consts}
        cross_q = {}
        xn1_free = [None]
        q1_free = [None, None]
        x_free = [None, None]

        def prepare_query(b):
            i = b % 2
            if b:
                x_ready[b] = x_loads[i].load(sp, lambda e: e.dma_start(x_in[:, i, :], x[b]), x_free[i])
            n = layernorm(0, x_in[:, i, :], xn1[:, :], x_ready[b], xn1_free[0])
            k, bank, free = ring_t.take()
            t = transpose4(bank, chunks(xn1), n, free, consts)
            xn1_free[0] = t
            ring_t.free[k] = hi_lo(bank, q1_hi[:, i, :], q1_lo[:, i, :], t, q1_free[i])
            cross_q[b] = ring_t.free[k]

        cross_out = {}
        prob_free, x1_free, o_free = [wc_split], [None], [None]

        def cross_attention(b):
            i, base = b % 2, b * 2 * NPT
            maxes = []
            for c in range(NCH):
                split_ahead(base + 2 * c + 4)
                k, bank, free = ring_s.take()
                for half in range(2):
                    n = base + 2 * c + half
                    s, (e_hi, e_lo) = next_piece(n)
                    for j in range(2):
                        kk = 2 * half + j
                        th, tl = hi[:, s, j * 512:(j + 1) * 512], lo[:, s, j * 512:(j + 1) * 512]
                        qh, ql = (q[:, i, kk * P:(kk + 1) * P] for q in (q1_hi, q1_lo))
                        mm(bank, qh, th, kk == 0, False, cross_q[b], free, e_hi)
                        mm(bank, qh, tl, False, False, e_lo)
                        last = mm(bank, ql, th, False, kk == 3, signal=j == 1)
                    split_free[s] = last
                q1_free[i] = last
                ring_s.free[k] = dve.do(lambda e, bank=bank, c=c: e.tensor_scalar(
                    prob[:, c * 512:(c + 1) * 512], bank, 1.0, None, ALU.mult, ALU.max,
                    accum_out=cmax[:, c:c + 1]), last, prob_free[0])
                maxes.append(ring_s.free[k])
                yield
            m = dve.do(lambda e: e.tensor_reduce(nmax[:, :], cmax[:, :], AX.X, ALU.max, negate=True), maxes[-1],
                       prob_free[0])
            exps = [act.do(lambda e, c=c: e.activation(
                prob[:, c * 512:(c + 1) * 512], prob[:, c * 512:(c + 1) * 512], ACT.Exp, bias=nmax[:, :],
                accum_out=rsum[:, c:c + 1]), m, o_free[0]) for c in range(NCH)]
            split_ahead(base + NPT + 2)
            yield
            r = dve.do(lambda e: e.tensor_reduce(rinv[:, 0:1], rsum[:, :], AX.X, ALU.add), exps[-1], o_free[0])
            r = dve.do(lambda e: e.reciprocal(rinv[:, 1:2], rinv[:, 0:1]), r)

            def transpose_probs(g):
                k, bank, free = ring_t.take()
                t = transpose4(bank, chunks(prob[:, g * 512:(g + 1) * 512]), exps[g], free)
                j, slot_, pfree = ring_p.take()
                ring_t.free[k] = hi_lo(bank, pT_hi[:, j, :], pT_lo[:, j, :], t, pfree)
                return j, ring_t.free[k], t

            ahead = transpose_probs(0)
            for g in range(NCH):
                split_ahead(base + NPT + 2 * g + 4)
                j, ready, t = ahead
                if g + 1 < NCH:
                    ahead = transpose_probs(g + 1)
                yield
                for half in range(2):
                    s, (e_hi, e_lo) = next_piece(base + NPT + 2 * g + half)
                    for u in range(2):
                        tile = 2 * half + u
                        vh, vl = hi[:, s, u * 512:(u + 1) * 512], lo[:, s, u * 512:(u + 1) * 512]
                        ph, pl = (p[:, j, tile * P:(tile + 1) * P] for p in (pT_hi, pT_lo))
                        first, end = g == 0 and tile == 0, g == NCH - 1 and tile == 3
                        mm(bank_o[:, :], ph, vh, first, False, ready, e_hi, o_free[0])
                        mm(bank_o[:, :], ph, vl, False, False, e_lo)
                        last = mm(bank_o[:, :], pl, vh, False, end, signal=u == 1)
                    split_free[s] = last
                ring_p.free[j] = last
            prob_free[0] = t
            o = dve.do(lambda e: e.scalar_tensor_tensor(x1[:, :], bank_o[:, :], rinv[:, 1:2], x_in[:, i, :],
                                                        ALU.mult, ALU.add), last, r, x1_free[0])
            o_free[0] = x_free[i] = cross_out[b] = o
            yield

        qk_free = qT_free = kbd_free = vp_free = t_free = xn_free = y_free = None
        heads = lambda ap: ap.rearrange("p (h d) -> p h d", d=DH)

        def project(banks, w_high, w_low, ready, *after):
            for c in range(KD):
                sh, sl = t_hi[:, c * P:(c + 1) * P], t_lo[:, c * P:(c + 1) * P]
                for st_, w in ((sh, w_high), (sh, w_low), (sl, w_high)):
                    for j, bank in enumerate(banks):
                        ev = mm(bank, st_, w[:, c, j * D:(j + 1) * D], c == 0 and st_ is sh and w is w_high,
                                c == KD - 1 and st_ is sl, ready, *after,
                                signal=c == KD - 1 and st_ is sl)
            return ev

        free = {}

        def self_attention_and_ffn(b):
            n = layernorm(1, x1[:, :], xn[:, :], cross_out[b], free.get("xn"))
            k, bank, bfree = ring_t.take()
            t = transpose4(bank, chunks(xn), n, bfree)
            free["xn"] = t
            tok = ring_t.free[k] = hi_lo(bank, t_hi[:, :], t_lo[:, :], t, free.get("t"))
            yield
            takes = [ring_a.take() for _ in range(3)]
            banks = [bk for _, bk, _ in takes]
            order = [i for i, _, _ in takes]
            done = project(banks, w_hi, w_lo, tok, folded, *[f for _, _, f in takes])
            free["t"] = done
            qb, kb, vb = banks
            for j, bk in ((0, qb), (1, kb)):
                src, dst = heads(bk), heads(qk[:, j, :])
                e_c = act.do(lambda e, src=src, dst=dst: e.activation(dst[:, :, 0:DHE], src[:, :, 0:DHE], ACT.Copy),
                             done, free.get("qk"))
                half = rope_b[:, j * H:(j + 1) * H, :]
                pair = lambda ap: ap.rearrange("p h (i two) -> p h i two", two=2)
                cos_b = cosb[:, :].unsqueeze(1).to_broadcast([P, H, DHE])
                sn = sinb[:, :].rearrange("p (i two) -> p i two", two=2)
                swaps = []
                for a in range(2):
                    swaps.append(dve.do(lambda e, a=a, src=src, half=half, sn=sn: e.tensor_tensor(
                        pair(half)[:, :, :, a], pair(src[:, :, DHE:DH])[:, :, :, 1 - a],
                        sn[:, :, a].unsqueeze(1).to_broadcast([P, H, DHE // 2]), ALU.mult),
                        e_c, free.get("rope")))
                e_m = dve.do(lambda e, src=src, dst=dst, cos_b=cos_b: e.tensor_tensor(
                    dst[:, :, DHE:DH], src[:, :, DHE:DH], cos_b, ALU.mult), e_c, free.get("qk"))
                ring_a.free[order[j]] = e_m
                e_r = dve.do(lambda e, dst=dst, half=half: e.tensor_tensor(
                    dst[:, :, DHE:DH], dst[:, :, DHE:DH], half, ALU.add), e_m, *swaps)
            free["rope"] = roped = e_r
            part = lambda i: vp[:, :, i * DH:(i + 1) * DH]
            a = act.do(lambda e: e.activation(part(2), heads(vb), ACT.Copy), done, free.get("vp"))
            a2 = ring_a.free[order[2]] = dve.do(lambda e: e.tensor_tensor(heads(v_res[:, :]), heads(vb), part(2),
                                                                        ALU.subtract), a, free.get("v_res"))
            a = act.do(lambda e: e.activation(part(1), heads(v_res[:, :]), ACT.Copy), a2, free.get("vp"))
            v_ready = pool.do(lambda e: e.tensor_tensor(part(0), heads(v_res[:, :]), part(1), ALU.subtract),
                              a, a2, free.get("vp"))
            free["v_res"] = v_ready
            yield
            k, bank, bfree = ring_t.take()
            t = transpose4(bank, chunks(qk[:, 0, :]), roped, e_c, bfree)
            q_ready = ring_t.free[k] = act.do(lambda e, bank=bank: e.activation(qT[:, :], bank, ACT.Copy), t,
                                              free.get("qT"))
            k, bank, bfree = ring_t.take()
            t = transpose4(bank, chunks(qk[:, 1, :]), bfree)
            free["qk"] = t
            for h in range(4):
                rows = slice(h * DH, (h + 1) * DH)
                k_ready = act.do(lambda e, h=h, rows=rows, bank=bank: e.activation(
                    kbd[rows, :, h * T:(h + 1) * T], bank[rows, :].rearrange("p (g t) -> p g t", g=HG), ACT.Copy),
                    t, free.get("kbd"), z_kbd)
            ring_t.free[k] = k_ready
            yield
            scale = DH ** -0.5

            def scores(g):
                i, bank, bfree = ring_a.take()
                e = mm(bank, qT[:, g * P:(g + 1) * P], kbd[:, g, :], True, True, q_ready, k_ready, bfree, signal=True)
                free["qT"] = free["kbd"] = e
                j, _, sfree = ring_sc.take()
                s3 = sc[:, j, :].rearrange("p (h t) -> p h t", h=4)
                a = ring_a.free[i] = dve.do(lambda en, s3=s3, bank=bank: en.tensor_tensor(
                    s3, bank.rearrange("p (h t) -> p h t", h=4),
                    mask[:, :].unsqueeze(1).to_broadcast([P, 4, T]), ALU.add), e, sfree)
                a = dve.do(lambda en, s3=s3, j=j: en.tensor_reduce(smax[:, j, :], s3, AX.X, ALU.max), a, sfree)
                a = pool.do(lambda en, s3=s3, j=j: en.tensor_tensor(
                    s3, s3, smax[:, j, :].unsqueeze(2).to_broadcast([P, 4, T]), ALU.subtract), a)
                a = act.do(lambda en, j=j: en.activation(sc[:, j, :], sc[:, j, :], ACT.Exp, scale=scale), a)
                return j, a

            def probs_transposed(j, ready):
                k, bank, bfree = ring_t.take()
                t = transpose4(bank, chunks(sc[:, j, :]), ready, bfree)
                ring_sc.free[j] = t
                m, _, pfree = ring_pp.take()
                hi_, mid_, lo_ = (p_part[:, m, i, :] for i in range(3))
                a = act.do(lambda e: e.activation(hi_, bank, ACT.Copy), t, pfree)
                b_ = ring_t.free[k] = dve.do(lambda e: e.tensor_tensor(p_res[:, :], bank, hi_, ALU.subtract), a,
                                             free.get("p_res"))
                c_ = act.do(lambda e: e.activation(mid_, p_res[:, :], ACT.Copy), b_)
                d_ = pool.do(lambda e: e.tensor_tensor(lo_, p_res[:, :], mid_, ALU.subtract), c_, b_)
                free["p_res"] = d_
                return m, d_

            def values(g, m, ready):
                i, bank, bfree = ring_a.take()
                for h in range(4):
                    for part_ in range(3):
                        o = bank[:, h * VW + part_ * DH:(h + 1) * VW]
                        e = mm(o, p_part[:, m, part_, h * T:(h + 1) * T], vp[:, 4 * g + h, part_ * DH:VW],
                               part_ == 0, part_ == 2, ready, v_ready, one_vp, bfree,
                               signal=h == 3 and part_ == 2)
                ring_pp.free[m] = e
                free["vp"] = e
                o4 = bank[:, 0:4 * VW].rearrange("p (h n) -> p h n", n=VW)
                y3 = heads(y[:, g * P:(g + 1) * P])
                r1 = dve.do(lambda en: en.reciprocal(sinv[:, :].unsqueeze(2), o4[:, :, 3 * DH:VW]), e, free.get("sinv"))
                r2 = ring_a.free[i] = dve.do(lambda en: en.tensor_reduce(
                    y3, o4[:, :, 0:3 * DH].rearrange("p h (i d) -> p h d i", i=3), AX.X, ALU.add), e, free.get("y"))
                r3 = dve.do(lambda en: en.tensor_tensor(y3, y3, sinv[:, :].unsqueeze(2).to_broadcast([P, 4, DH]),
                                                        ALU.mult), r1, r2)
                free["sinv"] = r3
                return r3

            sg = [scores(0), scores(1)]
            yield
            pg = probs_transposed(*sg[0])
            yield
            for g in range(HG):
                nxt = probs_transposed(*sg[g + 1]) if g + 1 < HG else None
                if g + 2 < HG:
                    sg.append(scores(g + 2))
                y_ready = values(g, *pg)
                pg = nxt
                yield
            k, bank, bfree = ring_t.take()
            t = transpose4(bank, chunks(y), y_ready, bfree)
            free["y"] = t
            tok = ring_t.free[k] = hi_lo(bank, t_hi[:, :], t_lo[:, :], t, free.get("t"))
            yield
            i, bank, bfree = ring_a.take()
            done = project([bank], wc_hi, wc_lo, tok, wc_split, bfree)
            free["t"] = done
            x2 = ring_a.free[i] = dve.do(lambda e, bank=bank: e.tensor_tensor(x1[:, :], bank, x1[:, :], ALU.add), done)
            n = layernorm(2, x1[:, :], xn[:, :], x2, free.get("xn"))
            xr = dve.do(lambda e: e.tensor_tensor(x1[:, :], x1[:, :], xn[:, :], ALU.add), n)
            yield
            k, bank, bfree = ring_t.take()
            t = transpose4(bank, chunks(xn), n, bfree)
            free["xn"] = t
            tT = ring_t.free[k] = act.do(lambda e, bank=bank: e.activation(qT[:, :], bank, ACT.Copy), t,
                                         free.get("qT"))
            yield
            i, bank, bfree = ring_a.take()
            for c in range(KD):
                e = mm(bank[:, 0:E], qT[:, c * P:c * P + 1].to_broadcast([P, P]), wr[:, c, :], c == 0, c == KD - 1,
                       tT, bfree, signal=c == KD - 1)
            a = dve.do(lambda en, bank=bank: en.max(top[:, :], bank[:, 0:E]), e, free.get("gate"))
            a = ring_a.free[i] = dve.do(lambda en, bank=bank: en.max_index(topi[:, :], top[:, :], bank[:, 0:E]), a,
                                        free.get("gate"))
            picked = a
            a = dve.do(lambda en: en.tensor_tensor(gt[:, 0:1], top[:, 1:2], top[:, 0:1], ALU.subtract), a,
                       free.get("gate"))
            a = act.do(lambda en: en.activation(gt[:, 1:2], gt[:, 0:1], ACT.Exp), a)
            a1 = dve.do(lambda en: en.tensor_scalar(gt[:, 2:3], gt[:, 1:2], 1.0, None, ALU.add), a)
            a1 = dve.do(lambda en: en.reciprocal(gt[:, 3:4], gt[:, 2:3]), a1)
            a2_ = dve.do(lambda en: en.tensor_scalar(gt[:, 4:5], gt[:, 1:2], slot[:, 0:1], slot[:, 1:2],
                                                     ALU.mult, ALU.add), a)
            gate = dve.do(lambda en: en.tensor_tensor(gt[:, 5:6], gt[:, 4:5], gt[:, 3:4], ALU.mult), a1, a2_)
            held = {}
            for k_ in range(2):
                def pick(en, k_=k_, held=held):
                    which = en.value_load(topi[0:1, k_:k_ + 1], min_val=0, max_val=E - 1)
                    held[k_] = which
                    return en.dma_start(ya[:, :, k_ * R:(k_ + 1) * R],
                                        expA[bass.ds(which, 1), :, :].rearrange("o p (c r) -> (o p) c r", r=R))

                def pick_b(en, k_=k_, held=held):
                    return en.dma_start(yb[k_ * R:(k_ + 1) * R, :],
                                        expB[bass.ds(held[k_], 1), :, :].rearrange("o p n -> (o p) n"))
                expert_loads.load(pool, pick, picked, free.get("experts"))
                experts = expert_loads.load(pool, pick_b, picked)
            yield
            yield
            i, bank, bfree = ring_a.take()
            for c in range(KD):
                e = mm(bank[:, 0:T], ya[:, c, :], qT[:, c * P:(c + 1) * P], c == 0, c == KD - 1, experts, bfree,
                       signal=c == KD - 1)
            free["qT"] = e
            m = ring_a.free[i] = dve.do(lambda en, bank=bank: en.tensor_scalar(midT[:, :], bank[:, 0:T], gt[:, 5:6],
                                                                              None, ALU.mult), e, gate,
                                        free.get("mid"))
            free["gate"] = m
            yield
            i, bank, bfree = ring_a.take()
            e = mm(bank, midT[:, :], yb[:, :], True, True, m, bfree, signal=True)
            free["experts"] = free["mid"] = e
            o = ring_a.free[i] = dve.do(lambda en, bank=bank: en.tensor_tensor(y[:, :], bank, x1[:, :], ALU.add), e,
                                        xr, free.get("y"))
            x1_free[0] = o
            free["y"] = stores.load(sp, lambda en: en.dma_start(out[b], y[:, :]), o)
            yield

        stage_free = None
        for j in range(3):
            ld = down_loads[j].load(sp, lambda e, j=j: e.dma_start(
                raw[:, 0:4, :].rearrange("p a n -> p (a n)").rearrange("p (g n) -> p g n", g=8),
                wdT[j].rearrange("(g p) n -> p g n", p=P)), stage_free)
            for c in range(KD):
                k, bank, bfree = ring_a.take()
                for g in range(8):
                    e = mm(bank[:, g * 64:(g + 1) * 64],
                           raw[:, g // 2, (g % 2) * 512 + c * P:(g % 2) * 512 + (c + 1) * P], up[:, j, :],
                           True, True, ld, consts, bfree, signal=g == 7)
                ring_a.free[k] = folded = hi_lo(bank, w_hi[:, c, j * D:(j + 1) * D], w_lo[:, c, j * D:(j + 1) * D], e)
            stage_free = e
        for r in range(RAW):
            raw_free[r] = e if r < 4 else None
        ring_sc.free = [e, e]

        for _ in range(RAW):
            send_piece()
        prepare_query(0)

        def step(gen):
            if gen is not None:
                next(gen, None)

        for b in range(NB + 1):
            main = cross_attention(b) if b < NB else None
            tail = self_attention_and_ffn(b - 1) if b else None
            steps = 0
            alive = True
            while alive:
                alive = False
                if tail is not None and next(tail, "end") != "end":
                    alive = True
                if tail is not None and steps >= 4 and next(tail, "end") != "end":
                    alive = True
                if main is not None and next(main, "end") != "end":
                    alive = True
                if steps == 4 and b + 1 < NB:
                    prepare_query(b + 1)
                steps += 1

        with nc.Block() as block:
            @block.sync
            def _(eng):
                sp.play(eng)
                eng.wait_ge(stores.sem, stores.count)

            @block.tensor
            def _(eng):
                pe.play(eng)

            @block.scalar
            def _(eng):
                act.play(eng)

            @block.vector
            def _(eng):
                dve.play(eng)

            @block.gpsimd
            def _(eng):
                pool.play(eng)


def kernel(x, ctx_1024, L0_attn_Wq_down, L0_attn_Wk_down, L0_attn_Wv_down, L0_attn_Wq_up_c, L0_attn_Wq_up_e,
           L0_attn_Wk_up_c, L0_attn_Wk_up_e, L0_attn_Wv_up, L0_attn_Wc, L0_ffn_Wr, L0_ffn_A, L0_ffn_Bw):
    import concourse.bacc as bacc
    from concourse.bass_utils import run_bass_kernel_spmd

    a = np.asarray
    ctx = a(ctx_1024)
    ctxT = ctx.reshape(NB, NCH, 512, 2, 2, P).transpose(0, 1, 3, 5, 4, 2).reshape(NB, NPT, P, PIECE)
    ctxN = ctx.reshape(NB, NPT, 2, P, D).transpose(0, 1, 3, 2, 4).reshape(NB, NPT, P, PIECE)
    inv_freq = (1.0 / np.float32(10000.0) ** (np.arange(0, DHE, 2, dtype=np.float32) / np.float32(DHE))).astype(np.float32)
    angle = np.arange(T, dtype=np.float32)[:, None] * inv_freq[None, :]
    angle = np.concatenate((angle, angle), axis=-1)
    sign = np.where(np.arange(DHE) % 2 == 0, -1.0, 1.0).astype(np.float32)
    arrays = {
        "x": a(x), "ctxT": ctxT, "ctxN": ctxN,
        "wdT": np.stack([a(w).T for w in (L0_attn_Wq_down, L0_attn_Wk_down, L0_attn_Wv_down)]),
        "wup_c": np.stack([a(L0_attn_Wq_up_c), a(L0_attn_Wk_up_c)]),
        "wup_e": np.stack([a(L0_attn_Wq_up_e), a(L0_attn_Wk_up_e)]),
        "wup_v": a(L0_attn_Wv_up), "wc": a(L0_attn_Wc),
        "routerT": a(L0_ffn_Wr).T.reshape(KD, P, E).transpose(1, 0, 2),
        "expA": a(L0_ffn_A).transpose(0, 2, 1).reshape(E, KD, P, R).transpose(0, 2, 1, 3).reshape(E, P, KD * R),
        "expB": a(L0_ffn_Bw).transpose(0, 2, 1),
        "cos_t": np.cos(angle), "sin_t": np.sin(angle) * sign,
        "mask_t": np.where(np.tril(np.ones((T, T), bool)), 0.0, MASK).astype(np.float32),
        "ident_t": np.eye(P, dtype=np.float32),
        "slot_t": np.stack([np.arange(P) >= R, np.arange(P) < R], axis=1).astype(np.float32),
    }
    nc = bacc.Bacc("TRN2", target_bir_lowering=False, num_devices=1)
    arrays = {k: np.ascontiguousarray(v) for k, v in arrays.items()}
    args = [nc.dram_tensor(k, v.shape, mybir.dt.from_np(v.dtype), kind="ExternalInput").ap() for k, v in arrays.items()]
    out = nc.dram_tensor("out", (NB, T, D), F32, kind="ExternalOutput").ap()
    perceiver(nc, *args, out)
    return run_bass_kernel_spmd(nc, [arrays], core_ids=[0]).results[0]["out"]
```

```python
import numpy as np
import concourse.bass as bass
from concourse import mybir
from contextlib import ExitStack

F32, F32R, BF16, U32 = mybir.dt.float32, mybir.dt.float32r, mybir.dt.bfloat16, mybir.dt.uint32
ALU, ACT, AX = mybir.AluOpType, mybir.ActivationFunctionType, mybir.AxisListType

P = 128
NB, T, D, S = 16, 128, 512, 2048
H, L, DH = 16, 64, 32
DHE = DH // 2
E, R = 8, 64
KD = D // P
NCH = S // 512
HG = H // 4
PIECE = 1024
NPT = 8
RAW, SPLIT, LOOK = 6, 5, 3
NWP = 14
HI_ENGINE, LO_ENGINE = "DAAAADAAAAAAAAAA", "DPDPDPDPPDPPDPPD"
SUB_ENGINE, LOW_ENGINE = "PDPP", "PPPP"
ORDER = "XXFAXXFAXFXAAAXAFXFAAXAQAXAAXXAAAXAXAXAXQAXA"
VW = 3 * DH + 1
EPS = 1e-5
MASK = -1e30


class Lane:

    def __init__(self, sem, step=1):
        self.sem, self.step, self.count, self.queue, self.waited = sem, step, 0, [], {}

    def do(self, make, *after, signal=True):
        waits = []
        for lane, value in filter(None, after):
            if self.waited.get(lane, 0) < value:
                self.waited[lane] = value
                waits.append((lane.sem, value))
        self.queue.append((waits, make, signal))
        self.count += signal
        return (self, self.count) if signal else None

    def play(self, eng):
        for waits, make, signal in self.queue:
            for sem, value in waits:
                eng.wait_ge(sem, value)
            made = make(eng)
            if signal:
                made.then_inc(self.sem, 1)


class Loads:

    def __init__(self, sem):
        self.sem, self.count = sem, 0

    def load(self, lane, make, *after):
        self.count += 16
        sem = self.sem
        lane.do(lambda e: make(e).then_inc(sem, 16), *after, signal=False)
        return (self, self.count)


def perceiver(nc, x, ctxT, ctx, wdT, wup_c, wup_e, wup_v, wc, wrT, expA, expB, cos_t, sin_t, mask_t, ident_t,
              slot_t, out):
    with ExitStack() as stack:
        def sb(name, shape, dt=F32):
            return stack.enter_context(nc.sbuf_tensor(name, shape, dt))

        def ps(name, shape, dt=F32):
            return stack.enter_context(nc.psum_tensor(name, shape, dt))

        def sem(name):
            return stack.enter_context(nc.semaphore(name))

        raw = sb("ctx_raw", [P, RAW, PIECE])
        hi = sb("ctx_high", [P, SPLIT, PIECE], F32R)
        lo = sb("ctx_low", [P, SPLIT, PIECE], F32R)
        prob = sb("cross_prob", [P, S])
        pT_hi = sb("cross_probT_high", [P, 2, 512], F32R)
        pT_lo = sb("cross_probT_low", [P, 2, 512], F32R)
        w_hi = sb("wqkv_high", [P, KD, 3 * D], F32R)
        w_lo = sb("wqkv_low", [P, KD, 3 * D], F32R)
        wc_hi = sb("wc_high", [P, KD, D], F32R)
        wc_lo = sb("wc_low", [P, KD, D], F32R)
        x_in = sb("x_in", [P, 2, D])
        x1s = sb("x1", [P, 2, D])
        xn = sb("x_normed", [P, D])
        xn1 = sb("x_normed_first", [P, D])
        xn3 = sb("x_normed_third", [P, D])
        tT3 = sb("ffn_tokensT", [P, D])
        q1_hi = sb("cross_qT_high", [P, D], F32R)
        q1_lo = sb("cross_qT_low", [P, D], F32R)
        t_hi = sb("tokensT_high", [P, D], F32R)
        t_lo = sb("tokensT_low", [P, D], F32R)
        qk = sb("qk_roped", [P, 2, D])
        rope_b = sb("rope_scratch", [P, 2 * H, DHE])
        qT = sb("qT", [P, D])
        kbd = sb("kT_block_diagonal", [P, HG, 512])
        vp = sb("v_parts", [P, H, VW], BF16)
        residue = sb("residue", [P, D])
        sc = sb("self_scores", [P, 2, 512])
        p_part = sb("self_probT_parts", [P, 2, 3, 512], BF16)
        y = sb("y", [P, D])
        ya = sb("expert_A", [P, KD, 2 * R])
        yb = sb("expert_B", [P, D])
        midT = sb("midT", [P, T])
        wr = sb("wrT", [P, KD, E])
        cosb = sb("rope_cos", [P, DHE])
        sinb = sb("sin_signed", [P, DHE])
        mask = sb("causal_mask", [P, T])
        ident = sb("identity", [P, P])
        slot = sb("second_expert", [P, 2])
        powm = sb("minus_half", [P, 1])
        st = sb("stats", [P, 3, 16])
        cmax = sb("cross_chunk_max", [P, NCH])
        nmax = sb("cross_neg_max", [P, 1])
        rsum = sb("cross_row_sums", [P, NCH])
        rinv = sb("cross_row_inverse", [P, 2])
        smax = sb("self_max", [P, 2, 4])
        sinv = sb("self_sum_inverse", [P, 4])
        top = sb("gate_top", [P, 8])
        topi = sb("gate_index", [P, 8], U32)
        gt = sb("gate_scratch", [P, 8])

        bank_s = [ps(f"bank_scores{i}", [P, 512]) for i in range(2)]
        bank_t = [ps(f"bank_transposed{i}", [P, 512]) for i in range(2)]
        bank_o = ps("bank_cross_out", [P, 512])
        bank_a = ps("banks_self", [P, 3, 512])

        pe, act, dve, pool, sp = (Lane(sem(n)) for n in ("pe", "act", "dve", "pool", "sp"))
        setup_loads = Loads(sem("setup_loads"))
        piece_loads = [Loads(sem(f"piece_loads{i}")) for i in range(RAW)]
        x_loads = [Loads(sem(f"x_loads{i}")) for i in range(2)]
        expert_loads = Loads(sem("expert_loads"))
        stores = Loads(sem("stores"))

        def f32(ap):
            return ap.bitcast(F32)

        def hi_lo(src, high, low, *after):
            e_hi = act.do(lambda e: e.activation(high, src, ACT.Copy), *after)
            return dve.do(lambda e: e.tensor_tensor(low, src, f32(high), ALU.subtract), e_hi, *after)

        def mm(o, a, b, start, stop, *after, signal=False, **kw):
            return pe.do(lambda e: e.matmul(o, a, b, start=start, stop=stop, **kw), *after, signal=signal)

        def transpose4(bank, tiles, *after):
            for i, tile in enumerate(tiles):
                ev = pe.do(lambda e, i=i, tile=tile: e.transpose(bank[:, i * P:(i + 1) * P], tile, ident[:, :]),
                           *after, signal=i == 3)
            return ev

        class Ring:

            def __init__(self, bufs):
                self.bufs, self.free, self.n = bufs, [None] * len(bufs), -1

            def take(self):
                self.n += 1
                self.i = self.n % len(self.bufs)
                return self.i, self.bufs[self.i], self.free[self.i]

        ring_t = Ring([b[:, :] for b in bank_t])
        ring_s = Ring([b[:, :] for b in bank_s])
        ring_a = Ring([bank_a[:, i, :] for i in range(3)])
        ring_p = Ring([0, 1])
        ring_sc = Ring([0, 1])
        ring_pp = Ring([0, 1])

        def load(dst, src, *after):
            return setup_loads.load(act, lambda e: e.dma_start(dst, src), *after)

        up = sc[:, 0, 0:384].rearrange("p (j n) -> p j n", j=3)
        z_up = dve.do(lambda e: e.memset(sc[:, 0, :], 0.0))
        z_kbd = pool.do(lambda e: e.memset(kbd[:, :, :], 0.0))
        c_pow = dve.do(lambda e: e.memset(powm[:, :], -0.5))
        one_vp = pool.do(lambda e: e.memset(vp[:, :, 3 * DH:VW], 1.0))
        x_first = x_loads[0].load(sp, lambda e: e.dma_start(x_in[:, 0, :], x[0]))
        identity = x_loads[1].load(act, lambda e: e.dma_start(ident[:, :], ident_t))
        for g in range(2):
            rows = slice(g * L, (g + 1) * L)
            for j in range(2):
                load(up[rows, j, g * DH:g * DH + DHE], wup_c[j], z_up)
                load(up[rows, j, g * DH + DHE:(g + 1) * DH], wup_e[j])
            load(up[rows, 2, g * DH:(g + 1) * DH], wup_v)
        load(cosb[:, :], cos_t)
        load(sinb[:, :], sin_t)
        load(mask[:, :], mask_t)
        load(slot[:, :], slot_t)
        consts = load(wr[:, :, :], wrT)

        raw_free, split_free = [None] * RAW, [None] * SPLIT
        arrived, split_done = {}, {}
        sent, split_next = [0], [0]

        def send_piece():
            n = sent[0]
            if n >= NWP + NB * 2 * NPT:
                return
            sent[0] += 1
            if n < 12:
                j, g = divmod(n, 4)
                src = wdT[j, g]
            elif n < NWP:
                src = wc[n - 12]
            else:
                b, i = divmod(n - NWP, 2 * NPT)
                src = ctxT[b, i] if i < NPT else ctx[b, i - NPT]
            r = n % RAW
            arrived[n] = piece_loads[r].load(sp, lambda e: e.dma_start(raw[:, r, :], src), raw_free[r])

        def split_piece(n):
            r, s = (n + NWP) % RAW, n % SPLIT
            came, i = arrived[n + NWP], n % (2 * NPT)
            if HI_ENGINE[i] == "A":
                e_hi = act.do(lambda e: e.activation(hi[:, s, :], raw[:, r, :], ACT.Copy), came, split_free[s])
            else:
                e_hi = dve.do(lambda e: e.tensor_copy(hi[:, s, :], raw[:, r, :]), came, split_free[s])
            lane = pool if LO_ENGINE[i] == "P" else dve
            e_lo = lane.do(lambda e: e.tensor_tensor(lo[:, s, :], raw[:, r, :], f32(hi[:, s, :]), ALU.subtract),
                           came, split_free[s], e_hi)
            raw_free[r] = e_lo
            send_piece()
            split_done[n] = (e_hi, e_lo)

        def next_piece(n):
            while split_next[0] <= min(n + LOOK, NB * 2 * NPT - 1):
                split_piece(split_next[0])
                split_next[0] += 1
            return n % SPLIT, split_done[n]

        stat_free = [None] * 3

        def layernorm(which, src, dst, ready, *dst_free):
            s = st[:, which, :]
            a = dve.do(lambda e: e.bn_stats(s[:, 0:6], src), ready, stat_free[which])
            a = dve.do(lambda e: e.bn_aggr(s[:, 8:10], s[:, 0:6]), a)
            a = dve.do(lambda e: e.tensor_scalar(s[:, 10:11], s[:, 9:10], EPS, None, ALU.add), a)
            a = pool.do(lambda e: e.tensor_tensor(s[:, 11:12], s[:, 10:11], powm[:, :], ALU.pow), a, c_pow)
            a = dve.do(lambda e: e.tensor_scalar(dst, src, s[:, 8:9], s[:, 11:12], ALU.subtract, ALU.mult), a, *dst_free)
            stat_free[which] = a
            return a

        def chunks(t):
            return [t[:, c * P:(c + 1) * P] for c in range(KD)]

        x_ready, cross_q, cross_out, free = {0: x_first}, {}, {}, {}

        def prepare_query(b):
            i = b % 2
            if b:
                x_ready[b] = x_loads[i].load(sp, lambda e: e.dma_start(x_in[:, i, :], x[b]), free.get(f"x{i}"))
            n = layernorm(0, x_in[:, i, :], xn1[:, :], x_ready[b], free.get("xn1"))
            yield
            k, bank, bfree = ring_t.take()
            t = transpose4(bank, chunks(xn1), n, bfree, identity)
            free["xn1"] = t
            cross_q[b] = ring_t.free[k] = hi_lo(bank, q1_hi[:, :], q1_lo[:, :], t, free.get("q1"))
            yield

        def cross_attention(b):
            i, base = b % 2, b * 2 * NPT
            for c in range(NCH):
                k, bank, bfree = ring_s.take()
                for half in range(2):
                    s, (e_hi, e_lo) = next_piece(base + 2 * c + half)
                    for j in range(2):
                        kk = 2 * half + j
                        th, tl = hi[:, s, j * 512:(j + 1) * 512], lo[:, s, j * 512:(j + 1) * 512]
                        qh, ql = (q[:, kk * P:(kk + 1) * P] for q in (q1_hi, q1_lo))
                        mm(bank, qh, th, kk == 0, False, cross_q[b], bfree, e_hi)
                        mm(bank, ql, th, False, False)
                        last = mm(bank, qh, tl, False, kk == 3, e_lo, signal=j == 1)
                    split_free[s] = last
                    if half == 0:
                        yield
                ring_s.free[k] = dve.do(lambda e, bank=bank, c=c: e.tensor_scalar(
                    prob[:, c * 512:(c + 1) * 512], bank, 1.0, None, ALU.mult, ALU.max,
                    accum_out=cmax[:, c:c + 1]), last, free.get("prob"))
                if c < NCH - 1:
                    yield
            free["q1"] = last
            m = dve.do(lambda e: e.tensor_reduce(nmax[:, :], cmax[:, :], AX.X, ALU.max, negate=True), ring_s.free[k],
                       free.get("prob"))
            exps = [act.do(lambda e, c=c: e.activation(
                prob[:, c * 512:(c + 1) * 512], prob[:, c * 512:(c + 1) * 512], ACT.Exp, bias=nmax[:, :],
                accum_out=rsum[:, c:c + 1]), m, free.get("out")) for c in range(NCH)]
            yield

            def transpose_probs(g):
                k, bank, bfree = ring_t.take()
                t = transpose4(bank, chunks(prob[:, g * 512:(g + 1) * 512]), exps[g], bfree)
                j, _, pfree = ring_p.take()
                ring_t.free[k] = hi_lo(bank, pT_hi[:, j, :], pT_lo[:, j, :], t, pfree)
                return j, ring_t.free[k], t

            ahead = transpose_probs(0)
            yield
            r = dve.do(lambda e: e.tensor_reduce(rinv[:, 0:1], rsum[:, :], AX.X, ALU.add), exps[-1], free.get("out"))
            r = dve.do(lambda e: e.reciprocal(rinv[:, 1:2], rinv[:, 0:1]), r)
            for g in range(NCH):
                j, ready, t = ahead
                if g + 1 < NCH:
                    ahead = transpose_probs(g + 1)
                for half in range(2):
                    s, (e_hi, e_lo) = next_piece(base + NPT + 2 * g + half)
                    for u in range(2):
                        tile = 2 * half + u
                        vh, vl = hi[:, s, u * 512:(u + 1) * 512], lo[:, s, u * 512:(u + 1) * 512]
                        ph, pl = (p[:, j, tile * P:(tile + 1) * P] for p in (pT_hi, pT_lo))
                        first, end = g == 0 and tile == 0, g == NCH - 1 and tile == 3
                        mm(bank_o[:, :], ph, vh, first, False, ready, e_hi, free.get("out"))
                        mm(bank_o[:, :], pl, vh, False, False)
                        last = mm(bank_o[:, :], ph, vl, False, end, e_lo, signal=u == 1)
                    split_free[s] = last
                    if (g, half) != (NCH - 1, 1):
                        yield
                ring_p.free[j] = last
            free["prob"] = t
            x1 = x1s[:, i, :]
            o = dve.do(lambda e: e.scalar_tensor_tensor(x1, bank_o[:, :], rinv[:, 1:2], x_in[:, i, :],
                                                        ALU.mult, ALU.add), last, r, free.get(f"x1{i}"))
            free["out"] = free[f"x{i}"] = o
            cross_out[b] = layernorm(1, x1, xn[:, :], o, free.get("xn"))
            yield

        heads = lambda ap: ap.rearrange("p (h d) -> p h d", d=DH)
        pairs = lambda ap: ap.rearrange("p h (i two) -> p h i two", two=2)

        def project(bank, w_high, w_low, col, *after):
            for c in range(KD):
                sh, sl = t_hi[:, c * P:(c + 1) * P], t_lo[:, c * P:(c + 1) * P]
                wh, wl = w_high[:, c, col:col + D], w_low[:, c, col:col + D]
                mm(bank, sh, wh, c == 0, False, *after)
                mm(bank, sh, wl, False, False)
                ev = mm(bank, sl, wh, False, c == KD - 1, signal=c == KD - 1)
            return ev

        def rope(j, bank, i, done):
            src, dst, rot = heads(bank), heads(qk[:, j, :]), rope_b[:, j * H:(j + 1) * H, :]
            e_c = act.do(lambda e: e.activation(dst[:, :, 0:DHE], src[:, :, 0:DHE], ACT.Copy), done, free.get("qk"))
            sn = sinb[:, :].rearrange("p (i two) -> p i two", two=2)
            for a in range(2):
                e_s = dve.do(lambda e, a=a: e.tensor_tensor(
                    pairs(rot)[:, :, :, a], pairs(src[:, :, DHE:DH])[:, :, :, 1 - a],
                    sn[:, :, a].unsqueeze(1).to_broadcast([P, H, DHE // 2]), ALU.mult), e_c, consts, free.get("rope"))
            e_m = dve.do(lambda e: e.tensor_tensor(
                dst[:, :, DHE:DH], src[:, :, DHE:DH], cosb[:, :].unsqueeze(1).to_broadcast([P, H, DHE]), ALU.mult),
                e_c, free.get("qk"))
            ring_a.free[i] = e_m
            return dve.do(lambda e: e.tensor_tensor(dst[:, :, DHE:DH], dst[:, :, DHE:DH], rot, ALU.add), e_m, e_s)

        def self_attention(b):
            x1 = x1s[:, b % 2, :]
            k, bank, bfree = ring_t.take()
            t = transpose4(bank, chunks(xn), cross_out[b], bfree)
            free["xn"] = t
            tok = ring_t.free[k] = hi_lo(bank, t_hi[:, :], t_lo[:, :], t, free.get("t"))
            yield
            roped = []
            for j in range(2):
                i, bank, bfree = ring_a.take()
                roped.append(rope(j, bank, i, project(bank, w_hi, w_lo, j * D, tok, folded[0], bfree)))
                yield
            free["rope"] = roped[1]
            i, bank, bfree = ring_a.take()
            free["t"] = done = project(bank, w_hi, w_lo, 2 * D, bfree)
            part = lambda n: vp[:, :, n * DH:(n + 1) * DH]
            vb = heads(bank)
            a = act.do(lambda e: e.activation(part(2), vb, ACT.Copy), done, free.get("vp"))
            a2 = ring_a.free[i] = dve.do(lambda e: e.tensor_tensor(heads(residue[:, :]), vb, part(2), ALU.subtract), a,
                                         free.get("residue"))
            a = act.do(lambda e: e.activation(part(1), heads(residue[:, :]), ACT.Copy), a2, free.get("vp"))
            free["residue"] = v_ready = pool.do(lambda e: e.tensor_tensor(
                part(0), heads(residue[:, :]), part(1), ALU.subtract), a, a2, free.get("vp"))
            yield
            k, bank_q, bfree = ring_t.take()
            t = transpose4(bank_q, chunks(qk[:, 0, :]), roped[0], bfree)
            q_ready = ring_t.free[k] = act.do(lambda e: e.activation(qT[:, :], bank_q, ACT.Copy), t, free.get("qT"))
            yield
            k, bank_k, bfree = ring_t.take()
            t = transpose4(bank_k, chunks(qk[:, 1, :]), roped[1], bfree)
            free["qk"] = t
            for h in range(4):
                rows = slice(h * DH, (h + 1) * DH)
                k_ready = act.do(lambda e, h=h, rows=rows: e.activation(
                    kbd[rows, :, h * T:(h + 1) * T], bank_k[rows, :].rearrange("p (g t) -> p g t", g=HG), ACT.Copy),
                    t, free.get("kbd"), z_kbd)
            ring_t.free[k] = k_ready
            yield
            scale = DH ** -0.5

            def scores(g):
                i, bank, bfree = ring_a.take()
                e = mm(bank, qT[:, g * P:(g + 1) * P], kbd[:, g, :], True, True, q_ready, k_ready, bfree, signal=True)
                free["qT"] = free["kbd"] = e
                j, _, sfree = ring_sc.take()
                s3 = sc[:, j, :].rearrange("p (h t) -> p h t", h=4)
                a = ring_a.free[i] = dve.do(lambda en: en.tensor_tensor(
                    s3, bank.rearrange("p (h t) -> p h t", h=4),
                    mask[:, :].unsqueeze(1).to_broadcast([P, 4, T]), ALU.add), e, consts, sfree)
                a = dve.do(lambda en: en.tensor_reduce(smax[:, j, :], s3, AX.X, ALU.max), a, sfree)
                lane = pool if SUB_ENGINE[g] == "P" else dve
                a = lane.do(lambda en: en.tensor_tensor(
                    s3, s3, smax[:, j, :].unsqueeze(2).to_broadcast([P, 4, T]), ALU.subtract), a)
                a = act.do(lambda en: en.activation(sc[:, j, :], sc[:, j, :], ACT.Exp, scale=scale), a)
                return j, a

            def probs_transposed(g, j, ready):
                k, bank, bfree = ring_t.take()
                t = transpose4(bank, chunks(sc[:, j, :]), ready, bfree)
                ring_sc.free[j] = t
                m, _, pfree = ring_pp.take()
                high, mid, low = (p_part[:, m, n, :] for n in range(3))
                a = act.do(lambda e: e.activation(high, bank, ACT.Copy), t, pfree)
                r = ring_t.free[k] = dve.do(lambda e: e.tensor_tensor(residue[:, :], bank, high, ALU.subtract), a,
                                            free.get("residue"))
                a = act.do(lambda e: e.activation(mid, residue[:, :], ACT.Copy), r)
                lane = pool if LOW_ENGINE[g] == "P" else dve
                free["residue"] = a = lane.do(lambda e: e.tensor_tensor(low, residue[:, :], mid, ALU.subtract), a, r)
                return m, a

            def values(g, m, ready):
                i, bank, bfree = ring_a.take()
                for h in range(4):
                    for n in range(3):
                        e = mm(bank[:, h * VW + n * DH:(h + 1) * VW], p_part[:, m, n, h * T:(h + 1) * T],
                               vp[:, 4 * g + h, n * DH:VW], n == 0, n == 2, ready, v_ready, one_vp, bfree,
                               signal=h == 3 and n == 2)
                ring_pp.free[m] = free["vp"] = e
                o4 = bank[:, 0:4 * VW].rearrange("p (h n) -> p h n", n=VW)
                y3 = heads(y[:, g * P:(g + 1) * P])
                r1 = dve.do(lambda en: en.reciprocal(sinv[:, :].unsqueeze(2), o4[:, :, 3 * DH:VW]), e, free.get("sinv"))
                r2 = ring_a.free[i] = dve.do(lambda en: en.tensor_reduce(
                    y3, o4[:, :, 0:3 * DH].rearrange("p h (i d) -> p h d i", i=3), AX.X, ALU.add), e, free.get("y"))
                free["sinv"] = r3 = dve.do(lambda en: en.tensor_tensor(
                    y3, y3, sinv[:, :].unsqueeze(2).to_broadcast([P, 4, DH]), ALU.mult), r1, r2)
                return r3

            s_, p_ = {}, {}
            for what in ("s0", "s1", "p0", "s2", "p1", "v0", "s3", "p2", "v1", "p3", "v2", "v3"):
                g = int(what[1])
                if what[0] == "s":
                    s_[g] = scores(g)
                elif what[0] == "p":
                    p_[g] = probs_transposed(g, *s_[g])
                else:
                    y_ready = values(g, *p_[g])
                yield
            k, bank, bfree = ring_t.take()
            free["y"] = t = transpose4(bank, chunks(y), y_ready, bfree)
            tok = ring_t.free[k] = hi_lo(bank, t_hi[:, :], t_lo[:, :], t, free.get("t"))
            yield
            i, bank_c, bfree = ring_a.take()
            free["t"] = done = project(bank_c, wc_hi, wc_lo, 0, tok, wc_split[0], bfree)
            x2 = ring_a.free[i] = dve.do(lambda e: e.tensor_tensor(x1, bank_c, x1, ALU.add), done)
            normed[b] = n = layernorm(2, x1, xn3[:, :], x2, free.get("xn3"))
            free["xn3r"] = residual[b] = dve.do(lambda e: e.tensor_tensor(x1, x1, xn3[:, :], ALU.add), n)
            yield

        normed, residual = {}, {}

        def ffn(b):
            x1 = x1s[:, b % 2, :]
            k, bank_t3, bfree = ring_t.take()
            t = transpose4(bank_t3, chunks(xn3), normed[b], bfree)
            free["xn3"] = t
            tT = ring_t.free[k] = act.do(lambda e: e.activation(tT3[:, :], bank_t3, ACT.Copy), t, free.get("tT3"))
            yield
            i, bank_l, bfree = ring_a.take()
            reps = P // E
            for c in range(KD):
                e = mm(bank_l[:, 0:P], tT3[:, c * P:c * P + 1].to_broadcast([P, P]),
                       wr[:, c, :].unsqueeze(1).to_broadcast([P, reps, E]), c == 0, c == KD - 1,
                       tT, bfree, signal=c == KD - 1)
            a = dve.do(lambda en: en.max(top[:, :], bank_l[:, 0:E]), e, free.get("gate"))
            a = ring_a.free[i] = picked = dve.do(
                lambda en: en.max_index(topi[:, :], top[:, :], bank_l[:, 0:E]), a, free.get("gate"))
            a = dve.do(lambda en: en.tensor_tensor(gt[:, 0:1], top[:, 1:2], top[:, 0:1], ALU.subtract), a,
                       free.get("gate"))
            a = act.do(lambda en: en.activation(gt[:, 1:2], gt[:, 0:1], ACT.Exp), a)
            a1 = dve.do(lambda en: en.tensor_scalar(gt[:, 2:3], gt[:, 1:2], 1.0, None, ALU.add), a)
            a1 = dve.do(lambda en: en.reciprocal(gt[:, 3:4], gt[:, 2:3]), a1)
            a2 = dve.do(lambda en: en.tensor_scalar(gt[:, 4:5], gt[:, 1:2], slot[:, 0:1], slot[:, 1:2],
                                                    ALU.mult, ALU.add), a)
            gate = dve.do(lambda en: en.tensor_tensor(gt[:, 5:6], gt[:, 4:5], gt[:, 3:4], ALU.mult), a1, a2)
            yield
            held = {}
            for n in range(2):
                def load_a(en, n=n):
                    held[n] = en.value_load(topi[0:1, n:n + 1], min_val=0, max_val=E - 1)
                    return en.dma_start(ya[:, :, n * R:(n + 1) * R],
                                        expA[bass.ds(held[n], 1), :, :].rearrange("o p (c r) -> (o p) c r", r=R))

                def load_b(en, n=n):
                    return en.dma_start(yb[n * R:(n + 1) * R, :],
                                        expB[bass.ds(held[n], 1), :, :].rearrange("o p n -> (o p) n"))
                expert_loads.load(pool, load_a, picked, free.get("experts"))
                experts = expert_loads.load(pool, load_b)
            yield
            i, bank_m, bfree = ring_a.take()
            for c in range(KD):
                e = mm(bank_m[:, 0:T], ya[:, c, :], tT3[:, c * P:(c + 1) * P], c == 0, c == KD - 1, experts, bfree,
                       signal=c == KD - 1)
            free["tT3"] = e
            m = ring_a.free[i] = dve.do(lambda en: en.tensor_scalar(midT[:, :], bank_m[:, 0:T], gt[:, 5:6],
                                                                    None, ALU.mult), e, gate, free.get("mid"))
            free["gate"] = m
            yield
            i, bank_f, bfree = ring_a.take()
            e = mm(bank_f, midT[:, :], yb[:, :], True, True, m, bfree, signal=True)
            free["experts"] = free["mid"] = e
            o = ring_a.free[i] = dve.do(lambda en: en.tensor_tensor(xn3[:, :], bank_f, x1, ALU.add), e,
                                        residual[b], free["xn3"])
            free[f"x1{b % 2}"] = o
            free["xn3"] = stores.load(sp, lambda en: en.dma_start(out[b], xn3[:, :]), o)
            yield

        for _ in range(RAW):
            send_piece()
        for _ in prepare_query(0):
            pass
        folded, wc_split = [None], [None]
        for j in range(3):
            slots = [(j * 4 + n) % RAW for n in range(4)]
            for c in range(KD):
                k, bank, bfree = ring_a.take()
                for g in range(8):
                    w = min(2 * 64, D - g * 64)
                    e = mm(bank[:, g * 64:g * 64 + w],
                           raw[:, slots[g // 2], (g % 2) * 512 + c * P:(g % 2) * 512 + (c + 1) * P],
                           up[:, j, 0:w], True, True, arrived[j * 4 + g // 2], consts, bfree,
                           signal=g == 7)
                ring_a.free[k] = folded[0] = hi_lo(bank, w_hi[:, c, j * D:(j + 1) * D],
                                                   w_lo[:, c, j * D:(j + 1) * D], e)
            for r in slots:
                raw_free[r] = e
                send_piece()
        ring_sc.free = [e, e]
        for n in range(2):
            r = (12 + n) % RAW
            src = raw[:, r, :].rearrange("p (k n) -> p k n", k=2)
            raw_free[r] = wc_split[0] = hi_lo(src, wc_hi[:, 2 * n:2 * n + 2, :], wc_lo[:, 2 * n:2 * n + 2, :],
                                              arrived[12 + n])
            send_piece()

        for b in range(NB + 2):
            work = {
                "X": cross_attention(b) if b < NB else None,
                "A": self_attention(b - 1) if 1 <= b <= NB else None,
                "F": ffn(b - 2) if b >= 2 else None,
                "Q": prepare_query(b + 1) if b + 1 < NB else None,
            }
            for what in ORDER:
                if work[what] is not None:
                    next(work[what], None)
            for gen in work.values():
                assert gen is None or next(gen, "end") == "end"

        with nc.Block() as block:
            @block.sync
            def _(eng):
                sp.play(eng)
                eng.wait_ge(stores.sem, stores.count)

            @block.tensor
            def _(eng):
                pe.play(eng)

            @block.scalar
            def _(eng):
                act.play(eng)

            @block.vector
            def _(eng):
                dve.play(eng)

            @block.gpsimd
            def _(eng):
                pool.play(eng)


def kernel(x, ctx_1024, L0_attn_Wq_down, L0_attn_Wk_down, L0_attn_Wv_down, L0_attn_Wq_up_c, L0_attn_Wq_up_e,
           L0_attn_Wk_up_c, L0_attn_Wk_up_e, L0_attn_Wv_up, L0_attn_Wc, L0_ffn_Wr, L0_ffn_A, L0_ffn_Bw):
    import concourse.bacc as bacc
    from concourse.bass_utils import run_bass_kernel_spmd

    a = np.asarray
    ctx = a(ctx_1024)
    ctxT = ctx.reshape(NB, NCH, 512, 2, 2, P).transpose(0, 1, 3, 5, 4, 2).reshape(NB, NPT, P, PIECE)
    ctxN = ctx.reshape(NB, NPT, 2, P, D).transpose(0, 1, 3, 2, 4).reshape(NB, NPT, P, PIECE)
    inv_freq = (1.0 / np.float32(10000.0) ** (np.arange(0, DHE, 2, dtype=np.float32) / np.float32(DHE))).astype(np.float32)
    angle = np.arange(T, dtype=np.float32)[:, None] * inv_freq[None, :]
    angle = np.concatenate((angle, angle), axis=-1)
    sign = np.where(np.arange(DHE) % 2 == 0, -1.0, 1.0).astype(np.float32)
    arrays = {
        "x": a(x), "ctxT": ctxT, "ctxN": ctxN,
        "wdT": np.stack([a(w).T.reshape(4, 2, P, D).transpose(0, 2, 1, 3).reshape(4, P, PIECE)
                         for w in (L0_attn_Wq_down, L0_attn_Wk_down, L0_attn_Wv_down)]),
        "wup_c": np.stack([a(L0_attn_Wq_up_c), a(L0_attn_Wk_up_c)]),
        "wup_e": np.stack([a(L0_attn_Wq_up_e), a(L0_attn_Wk_up_e)]),
        "wup_v": a(L0_attn_Wv_up), "wc": a(L0_attn_Wc).reshape(2, 2, P, D).transpose(0, 2, 1, 3).reshape(2, P, PIECE),
        "routerT": a(L0_ffn_Wr).T.reshape(KD, P, E).transpose(1, 0, 2),
        "expA": a(L0_ffn_A).transpose(0, 2, 1).reshape(E, KD, P, R).transpose(0, 2, 1, 3).reshape(E, P, KD * R),
        "expB": a(L0_ffn_Bw).transpose(0, 2, 1),
        "cos_t": np.cos(angle), "sin_t": np.sin(angle) * sign,
        "mask_t": np.where(np.tril(np.ones((T, T), bool)), 0.0, MASK).astype(np.float32),
        "ident_t": np.eye(P, dtype=np.float32),
        "slot_t": np.stack([np.arange(P) >= R, np.arange(P) < R], axis=1).astype(np.float32),
    }
    nc = bacc.Bacc("TRN2", target_bir_lowering=False, num_devices=1)
    arrays = {k: np.ascontiguousarray(v) for k, v in arrays.items()}
    args = [nc.dram_tensor(k, v.shape, mybir.dt.from_np(v.dtype), kind="ExternalInput").ap() for k, v in arrays.items()]
    out = nc.dram_tensor("out", (NB, T, D), F32, kind="ExternalOutput").ap()
    perceiver(nc, *args, out)
    return run_bass_kernel_spmd(nc, [arrays], core_ids=[0]).results[0]["out"]
```

```python
import numpy as np
import concourse.bass as bass
from concourse import mybir
from contextlib import ExitStack
from itertools import chain

F32, F32R, BF16, U32 = mybir.dt.float32, mybir.dt.float32r, mybir.dt.bfloat16, mybir.dt.uint32
ALU, ACT, AX = mybir.AluOpType, mybir.ActivationFunctionType, mybir.AxisListType

P = 128
NB, T, D, S = 16, 128, 512, 2048
H, L, DH = 16, 64, 32
DHE = DH // 2
E, R = 8, 64
KD = D // P
NCH = S // 512
HG = H // 4
PIECE = 1024
NPT = 8
X1 = 2
RAW, SPLIT, LOOK = 6, 5, 3
NWP = 14
FIRST_PIECES = "cccc" + "wc" * 12 + "ww"
HI_ENGINE, LO_ENGINE = "DAAEADAAAAAAAAAA", "DPDPDDDPEDPEPPPD"
KBD_ENGINE, LOW_ENGINE = "AAAA", "PEEP"
ENGINES = {"high": "A", "rope copy": "A", "rope sum": "P", "v low": "D", "p high": "D", "p middle": "A",
           "y": "E", "x2 sum": "D"}
B_STEPS = ("s0", "s1", "p0", "s2", "p1", "v0", "s3", "p2", "v1", "p3", "v2", "v3")
START = "XWXWXWWXXXWXWWXWQXXQXWWXWXWXWWXXX"
ROUND = "XAFXXXFAXFAAAXFAXFBQXXBBBXBBBXBBXBXXXBQBBXXB"
LAG = {"X": 0, "Q": 0, "A": 1, "B": 1, "F": 2}
LANES = {"pe": (0, 0.42, 0), "act": (0, 1.012, 100), "dve": (60, 1.06, 0), "pool": (60, 2.1, 1050), "sp": (50, 0, 50)}
SIGNAL_NS, TRANSFER_NS, DMA_NS = 130, 1450, 2000
WINDOW, PATIENCE, PE_PATIENCE, LATE = 10, 300, 950, 760
SPARE = {"dve": 0}
CONST_AT = [int(n) for n in np.cumsum([0, DHE, DHE, T, 2, KD * E])]
VW = 3 * DH + 1
EPS = 1e-5
MASK = -1e30


class Task:

    def __init__(self, makes, after, follows, sem, ns):
        self.makes, self.sem, self.value, self.ns = makes, sem, None, ns
        self.after = [t for group in after if group for t in (group if isinstance(group, tuple) else (group,)) if t]
        self.follows = [t for t in follows if t]


class Lane:

    def __init__(self, name, sem, fixed_ns, element_ns, dma_ns, program):
        self.name, self.sem = name, sem
        self.fixed_ns, self.element_ns, self.dma_ns = fixed_ns, element_ns, dma_ns
        self.program, self.queue = program, []

    def add(self, task):
        self.program.append(task)
        return task

    def do(self, make, *after, n=512, other=None, other_make=None, other_n=None, where="E", follows=(),
           signal=True):
        makes, ns = {self: make}, {self: self.fixed_ns + n * self.element_ns}
        if other and where != self.name[0].upper():
            makes[other] = other_make or make
            ns[other] = other.fixed_ns + (other_n or n) * other.element_ns
            if where != "E":
                del makes[self]
        return self.add(Task(makes, after, follows, list(makes)[0].sem if signal else None, ns))

    def number(self):
        for value, task in enumerate((t for t in self.queue if t.sem is self.sem), 1):
            task.value = value

    def play(self, eng):
        waited = {}
        for task in self.queue:
            waits = {}
            for event in task.after:
                waits[event.sem] = max(waits.get(event.sem, 0), event.value)
            for sem, value in waits.items():
                if waited.get(sem, 0) < value:
                    waited[sem] = value
                    eng.wait_ge(sem, value)
            made = task.makes[self](eng)
            if task.sem is self.sem:
                made.then_inc(self.sem, 1)


class Loads:

    def __init__(self, sem):
        self.sem, self.count, self.last = sem, 0, None

    def load(self, lane, make, *after):
        self.count += 16
        self.last = lane.add(Task({lane: lambda e: make(e).then_inc(self.sem, 16)}, after, (self.last,), self.sem,
                                  {lane: lane.dma_ns}))
        self.last.value = self.count
        return self.last


def arrange(lanes, program, work_of):
    pe = lanes[0]
    users = {t: [] for t in program}
    for t in program:
        for event in t.after + t.follows:
            users[event].append(t)
    need, place = {}, 0
    for t in program:
        need[t] = place if pe in t.makes else place + LATE
        place += pe in t.makes
    for t in reversed(program):
        need[t] = min([need[t]] + [need[u] for u in users[t]])
    runs, run = {}, []
    for t in program:
        if pe in t.makes:
            run.append(t)
            if t.sem:
                runs.setdefault(work_of[t], []).append(run)
                run = []
    rest = {lane: [t for t in program if lane in t.makes] for lane in lanes[1:]}
    free_at = {lane: 0.0 for lane in lanes}
    begun, done, link_free = set(), {}, 0.0

    def choices(lane):
        if lane is pe:
            near = [queue[0] for queue in runs.values() if queue]
        else:
            near = [[t] for t in rest[lane][:1 if lane is lanes[-1] else WINDOW]]
        for i, tasks in enumerate(near):
            if all(event in done for t in tasks for event in t.after) and \
                    all(x in begun for t in tasks for x in t.follows):
                start, offset = free_at[lane], 0.0
                for t in tasks:
                    start = max([start] + [done[event] - offset for event in t.after])
                    offset += t.ns[lane]
                t, cost = tasks[0], start + offset + SPARE.get(lane.name, 0)
                others = [max([free_at[x]] + [done[event] for event in t.after]) + t.ns[x] + SPARE.get(x.name, 0)
                          for x in t.makes if x is not lane]
                if cost <= min(others, default=cost):
                    yield start, min(need[t] for t in tasks), i, tasks

    def best(lane):
        options = list(choices(lane))
        limit = min((o[0] for o in options), default=0) + (PE_PATIENCE if lane is pe else PATIENCE)
        return min((o for o in options if o[0] <= limit), key=lambda o: (o[1], o[0]), default=None)

    picks = {lane: best(lane) for lane in lanes}
    left = len(program)
    while left:
        lane = min((lane for lane in lanes if picks[lane]), key=lambda lane: picks[lane][0])
        start, _, _, tasks = picks[lane]
        changed = {lane}
        last = tasks[-1]
        if lane is pe:
            runs[work_of[last]].pop(0)
        else:
            for x in last.makes:
                rest[x].remove(last)
                changed.add(x)
        lane.queue += tasks
        left -= len(tasks)
        begun.update(tasks)
        free_at[lane] = start + sum(t.ns[lane] for t in tasks)
        if last.sem in [x.sem for x in last.makes]:
            last.sem = lane.sem
            done[last] = free_at[lane] + SIGNAL_NS
        else:
            link_free = max(link_free, start) + TRANSFER_NS
            done[last] = max(link_free, free_at[lane] + DMA_NS)
        for u in users[last]:
            changed.update(u.makes)
        for x in lanes[1:4]:
            changed.add(x)
        for x in changed:
            picks[x] = best(x)


def order_of_rounds():
    rounds = NB + max(LAG.values())
    return START + "".join(w for r in range(1, rounds) for w in ROUND
                   if 0 <= r - LAG[w] < NB - (w == "Q"))


def perceiver(nc, x, ctxT, ctx, wdT, up, wc, expA, expB, const_t, ident_t, out):
    with ExitStack() as stack:
        def sb(name, shape, dt=F32):
            return stack.enter_context(nc.sbuf_tensor(name, shape, dt))

        def ps(name, shape, dt=F32):
            return stack.enter_context(nc.psum_tensor(name, shape, dt))

        def sem(name):
            return stack.enter_context(nc.semaphore(name))

        raw = sb("ctx_raw", [P, RAW, PIECE])
        hi = sb("ctx_high", [P, SPLIT, PIECE], F32R)
        lo = sb("ctx_low", [P, SPLIT, PIECE], F32R)
        prob = sb("cross_prob", [P, S])
        pT_hi = sb("cross_probT_high", [P, 2, 512], F32R)
        pT_lo = sb("cross_probT_low", [P, 2, 512], F32R)
        w_hi = sb("wqkv_high", [P, KD, 3 * D], F32R)
        w_lo = sb("wqkv_low", [P, KD, 3 * D], F32R)
        wc_hi = sb("wc_high", [P, KD, D], F32R)
        wc_lo = sb("wc_low", [P, KD, D], F32R)
        x_in = sb("x_in", [P, 2, D])
        x1s = sb("x1", [P, X1, D])
        xn = sb("x_normed", [P, D])
        xn1 = sb("x_normed_first", [P, D])
        xn3 = sb("x_normed_third", [P, D])
        tT3 = sb("ffn_tokensT", [P, D])
        q1_hi = sb("cross_qT_high", [P, D], F32R)
        q1_lo = sb("cross_qT_low", [P, D], F32R)
        t_hi = sb("tokensT_high", [P, D], F32R)
        t_lo = sb("tokensT_low", [P, D], F32R)
        qk = sb("qk_roped", [P, 2, D])
        rope_b = sb("rope_scratch", [P, 2 * H, DHE])
        qT = sb("qT", [P, D])
        kbd = sb("kT_block_diagonal", [P, HG, 512])
        vp = sb("v_parts", [P, H, VW], BF16)
        residue = sb("residue", [P, D])
        sc = sb("self_scores", [P, 2, 512])
        p_part = sb("self_probT_parts", [P, 2, 3, 512], BF16)
        y = sb("y", [P, D])
        ya = sb("expert_A", [P, KD, 2 * R])
        yb = sb("expert_B", [P, D])
        midT = sb("midT", [P, T])
        const = sb("constants", [P, 2 * DHE + T + 2 + KD * E])
        cosb, sinb, mask, slot, wr = (const[:, a:b] for a, b in zip(CONST_AT, CONST_AT[1:]))
        ident = sb("identity", [P, P])
        powm = sb("minus_half", [P, 1])
        st = sb("stats", [P, 3, 16])
        cmax = sb("cross_chunk_max", [P, NCH])
        nmax = sb("cross_neg_max", [P, 1])
        rsum = sb("cross_row_sums", [P, NCH])
        rinv = sb("cross_row_inverse", [P, 2])
        smax = sb("self_max", [P, 2, 4])
        sinv = sb("self_sum_inverse", [P, 4])
        top = sb("gate_top", [P, 8])
        topi = sb("gate_index", [P, 8], U32)
        gt = sb("gate_scratch", [P, 8])

        bank_s = [ps(f"bank_scores{i}", [P, 512]) for i in range(2)]
        bank_t = [ps(f"bank_transposed{i}", [P, 512]) for i in range(2)]
        bank_o = ps("bank_cross_out", [P, 512])
        bank_a = ps("banks_self", [P, 3, 512])

        program = []
        pe, act, dve, pool, sp = lanes = [Lane(name, sem(name), *ns, program) for name, ns in LANES.items()]
        setup_loads = Loads(sem("setup_loads"))
        piece_loads = [Loads(sem(f"piece_loads{i}")) for i in range(RAW)]
        x_loads = [Loads(sem(f"x_loads{i}")) for i in range(2)]
        expert_loads = Loads(sem("expert_loads"))
        stores = Loads(sem("stores"))

        def f32(ap):
            return ap.bitcast(F32)

        def hi_lo(src, high, low, *after, n=512):
            e_hi = act.do(lambda e: e.activation(high, src, ACT.Copy), *after, n=n,
                          other=dve, other_make=lambda e: e.tensor_copy(high, src), where=ENGINES["high"])
            return dve.do(lambda e: e.tensor_tensor(low, src, f32(high), ALU.subtract), e_hi, *after, n=n)

        def mm(o, a, b, start, stop, *after, signal=False, n=512):
            return pe.do(lambda e: e.matmul(o, a, b, start=start, stop=stop), *after, signal=signal, n=n)

        def transpose4(bank, tiles, *after):
            for i, tile in enumerate(tiles):
                ev = pe.do(lambda e, i=i, tile=tile: e.transpose(bank[:, i * P:(i + 1) * P], tile, ident[:, :]),
                           *after, signal=i == 3, n=256)
            return ev

        class Ring:

            def __init__(self, bufs):
                self.bufs, self.free, self.n = bufs, [None] * len(bufs), -1

            def take(self):
                self.n += 1
                i = self.n % len(self.bufs)
                after, self.free[i] = self.free[i], "in use"
                assert after != "in use", "its last reader isn't queued yet"
                return i, self.bufs[i], after

        ring_t = Ring([b[:, :] for b in bank_t])
        ring_s = Ring([b[:, :] for b in bank_s])
        ring_a = Ring([bank_a[:, i, :] for i in range(3)])
        ring_p = Ring([0, 1])
        ring_sc = Ring(list(range(2)))
        ring_pp = Ring(list(range(2)))

        def load(dst, src, *after):
            return setup_loads.load(act, lambda e: e.dma_start(dst, src), *after)

        up_at = [64 + 128 * j for j in range(3)]
        z_kbd = pool.do(lambda e: e.memset(kbd[:, :, :], 0.0))
        c_pow = dve.do(lambda e: e.memset(powm[:, :], -0.5))
        one_vp = pool.do(lambda e: e.memset(vp[:, :, 3 * DH:VW], 1.0))
        x_first = x_loads[0].load(sp, lambda e: e.dma_start(x_in[:, 0, :], x[0]))
        identity = x_loads[1].load(act, lambda e: e.dma_start(ident[:, :], ident_t))
        load(sc[:, 0, :], up)
        consts = load(const[:, :], const_t)

        raw_free, split_free = [None] * RAW, [None] * SPLIT
        stream, place = [], {}
        for kind in FIRST_PIECES + "c" * (NB * 2 * NPT - FIRST_PIECES.count("c")):
            piece = (kind, sum(1 for k, _ in stream if k == kind))
            place[piece] = len(stream)
            stream.append(piece)
        arrived, split_done, used = {}, {}, set()
        sent, split_next = [0], [0]

        def send_pieces():
            while sent[0] < len(stream) and (sent[0] < RAW or sent[0] - RAW in used):
                kind, n = stream[sent[0]]
                if kind == "c":
                    b, i = divmod(n, 2 * NPT)
                    src = ctxT[b, i] if i < NPT else ctx[b, i - NPT]
                else:
                    src = wdT[n // 4, n % 4] if n < 12 else wc[n - 12]
                r = sent[0] % RAW
                arrived[kind, n] = piece_loads[r].load(
                    sp, lambda e, r=r, src=src: e.dma_start(raw[:, r, :], src), raw_free[r])
                sent[0] += 1

        def used_piece(piece, event):
            raw_free[place[piece] % RAW] = event
            used.add(place[piece])
            send_pieces()

        def split_piece(n):
            r, s = place["c", n] % RAW, n % SPLIT
            came, i = arrived["c", n], n % (2 * NPT)
            e_hi = act.do(lambda e: e.activation(hi[:, s, :], raw[:, r, :], ACT.Copy), came, split_free[s], n=PIECE,
                          other=dve, other_make=lambda e: e.tensor_copy(hi[:, s, :], raw[:, r, :]),
                          other_n=PIECE * 5 // 8, where=HI_ENGINE[i])
            e_lo = pool.do(lambda e: e.tensor_tensor(lo[:, s, :], raw[:, r, :], f32(hi[:, s, :]), ALU.subtract),
                           came, split_free[s], e_hi, n=PIECE, other=dve, where=LO_ENGINE[i])
            used_piece(("c", n), e_lo)
            split_done[n] = (e_hi, e_lo)

        def next_piece(n):
            while split_next[0] <= min(n + LOOK, NB * 2 * NPT - 1):
                split_piece(split_next[0])
                split_next[0] += 1
            return n % SPLIT, split_done[n]

        stat_free = [None] * 3

        def layernorm(which, src, dst, ready, *dst_free):
            s = st[:, which, :]
            a = dve.do(lambda e: e.bn_stats(s[:, 0:6], src), ready, stat_free[which])
            a = dve.do(lambda e: e.bn_aggr(s[:, 8:10], s[:, 0:6]), a, n=8)
            a = dve.do(lambda e: e.tensor_scalar(s[:, 10:11], s[:, 9:10], EPS, None, ALU.add), a, n=1)
            a = pool.do(lambda e: e.tensor_tensor(s[:, 11:12], s[:, 10:11], powm[:, :], ALU.pow), a, c_pow, n=200)
            a = dve.do(lambda e: e.tensor_scalar(dst, src, s[:, 8:9], s[:, 11:12], ALU.subtract, ALU.mult), a, *dst_free)
            stat_free[which] = a
            return a

        def chunks(t):
            return [t[:, c * P:(c + 1) * P] for c in range(KD)]

        planned = set()

        def must(*milestone):
            assert milestone[-1] < 0 or milestone in planned, milestone

        x_ready, cross_q, cross_out, free = {0: x_first}, {}, {}, {}

        def prepare_query(b):
            i = b % 2
            must("crossed", b - 2)
            if b:
                x_ready[b] = x_loads[i].load(sp, lambda e: e.dma_start(x_in[:, i, :], x[b]), free.get(f"x{i}"))
            n = layernorm(0, x_in[:, i, :], xn1[:, :], x_ready[b], free.get("xn1"))
            yield
            must("scored", b - 1)
            k, bank, bfree = ring_t.take()
            t = transpose4(bank, chunks(xn1), n, bfree, identity)
            free["xn1"] = t
            cross_q[b] = ring_t.free[k] = hi_lo(bank, q1_hi[:, :], q1_lo[:, :], t, free.get("q1"))
            planned.add(("query", b))
            yield

        def cross_attention(b):
            i, base, chunk_max = b % 2, b * 2 * NPT, {}
            must("query", b)
            for c in range(NCH):
                k, bank, bfree = ring_s.take()
                for half in range(2):
                    s, (e_hi, e_lo) = next_piece(base + 2 * c + half)
                    for j in range(2):
                        kk = 2 * half + j
                        th, tl = hi[:, s, j * 512:(j + 1) * 512], lo[:, s, j * 512:(j + 1) * 512]
                        qh, ql = (q[:, kk * P:(kk + 1) * P] for q in (q1_hi, q1_lo))
                        mm(bank, qh, th, kk == 0, False, cross_q[b], bfree, e_hi)
                        mm(bank, ql, th, False, False)
                        last = mm(bank, qh, tl, False, kk == 3, e_lo, signal=j == 1)
                    split_free[s] = last
                    if half == 0:
                        yield
                ring_s.free[k] = chunk_max[c] = dve.do(lambda e, bank=bank, c=c: e.tensor_scalar(
                    prob[:, c * 512:(c + 1) * 512], bank, 1.0, None, ALU.mult, ALU.max,
                    accum_out=cmax[:, c:c + 1]), last, free.get("prob"))
                if c < NCH - 1:
                    yield
            free["q1"] = last
            planned.add(("scored", b))
            m = dve.do(lambda e: e.tensor_reduce(nmax[:, :], cmax[:, :], AX.X, ALU.max, negate=True),
                       *chunk_max.values(), free.get("prob"), n=4)
            exps = [act.do(lambda e, c=c: e.activation(
                prob[:, c * 512:(c + 1) * 512], prob[:, c * 512:(c + 1) * 512], ACT.Exp, bias=nmax[:, :],
                accum_out=rsum[:, c:c + 1]), m, free.get("out")) for c in range(NCH)]
            yield

            def transpose_probs(g):
                k, bank, bfree = ring_t.take()
                t = transpose4(bank, chunks(prob[:, g * 512:(g + 1) * 512]), exps[g], bfree)
                j, _, pfree = ring_p.take()
                ring_t.free[k] = hi_lo(bank, pT_hi[:, j, :], pT_lo[:, j, :], t, pfree)
                return j, ring_t.free[k], t

            ahead = transpose_probs(0)
            yield
            r = dve.do(lambda e: e.tensor_reduce(rinv[:, 0:1], rsum[:, :], AX.X, ALU.add), *exps, free.get("out"), n=4)
            r = dve.do(lambda e: e.reciprocal(rinv[:, 1:2], rinv[:, 0:1]), r, n=1)
            for g in range(NCH):
                j, ready, t = ahead
                if g + 1 < NCH:
                    ahead = transpose_probs(g + 1)
                for half in range(2):
                    s, (e_hi, e_lo) = next_piece(base + NPT + 2 * g + half)
                    for u in range(2):
                        tile = 2 * half + u
                        vh, vl = hi[:, s, u * 512:(u + 1) * 512], lo[:, s, u * 512:(u + 1) * 512]
                        ph, pl = (p[:, j, tile * P:(tile + 1) * P] for p in (pT_hi, pT_lo))
                        first, end = g == 0 and tile == 0, g == NCH - 1 and tile == 3
                        mm(bank_o[:, :], ph, vh, first, False, ready, e_hi, free.get("out"))
                        mm(bank_o[:, :], pl, vh, False, False)
                        last = mm(bank_o[:, :], ph, vl, False, end, e_lo, signal=u == 1)
                    split_free[s] = last
                    if (g, half) != (NCH - 1, 1):
                        yield
                ring_p.free[j] = last
            free["prob"] = t
            must("ffn", b - X1)
            must("normed tokens read", b - 1)
            x1 = x1s[:, b % X1, :]
            o = dve.do(lambda e: e.scalar_tensor_tensor(x1, bank_o[:, :], rinv[:, 1:2], x_in[:, i, :],
                                                        ALU.mult, ALU.add), last, r, free.get(f"x1{b % X1}"))
            free["out"] = free[f"x{i}"] = o
            cross_out[b] = layernorm(1, x1, xn[:, :], o, free.get("xn"))
            planned.add(("crossed", b))
            yield

        heads = lambda ap: ap.rearrange("p (h d) -> p h d", d=DH)
        pairs = lambda ap: ap.rearrange("p h (i two) -> p h i two", two=2)

        def project(bank, w_high, w_low, col, *after):
            for c in range(KD):
                sh, sl = t_hi[:, c * P:(c + 1) * P], t_lo[:, c * P:(c + 1) * P]
                wh, wl = w_high[:, c, col:col + D], w_low[:, c, col:col + D]
                mm(bank, sh, wh, c == 0, False, *after)
                mm(bank, sh, wl, False, False)
                ev = mm(bank, sl, wh, False, c == KD - 1, signal=c == KD - 1)
            return ev

        def rope(j, bank, i, done):
            src, dst, rot = heads(bank), heads(qk[:, j, :]), rope_b[:, j * H:(j + 1) * H, :]
            e_c = act.do(lambda e: e.activation(dst[:, :, 0:DHE], src[:, :, 0:DHE], ACT.Copy), done, free.get("qk"),
                         n=256, other=dve, other_make=lambda e: e.tensor_copy(dst[:, :, 0:DHE], src[:, :, 0:DHE]),
                         where=ENGINES["rope copy"])
            sn = sinb[:, :].rearrange("p (i two) -> p i two", two=2)
            e_s = None
            for a in range(2):
                e_s = dve.do(lambda e, a=a: e.tensor_tensor(
                    pairs(rot)[:, :, :, a], pairs(src[:, :, DHE:DH])[:, :, :, 1 - a],
                    sn[:, :, a].unsqueeze(1).to_broadcast([P, H, DHE // 2]), ALU.mult), e_c, consts, free.get(f"rope{j}"),
                    follows=(e_s,), n=128)
            e_m = dve.do(lambda e: e.tensor_tensor(
                dst[:, :, DHE:DH], src[:, :, DHE:DH], cosb[:, :].unsqueeze(1).to_broadcast([P, H, DHE]), ALU.mult),
                e_c, free.get("qk"), follows=(e_s,), n=256)
            ring_a.free[i] = e_m
            free[f"rope{j}"] = r = dve.do(lambda e: e.tensor_tensor(dst[:, :, DHE:DH], dst[:, :, DHE:DH], rot, ALU.add),
                                          e_m, e_s, n=256, other=pool, where=ENGINES["rope sum"])
            return r

        def projections(b):
            must("crossed", b)
            must("weights", 0)
            k, bank, bfree = ring_t.take()
            t = transpose4(bank, chunks(xn), cross_out[b], bfree)
            free["xn"] = t
            assert not free.get("t busy"), "tokensT is still to be read"
            free["t busy"] = True
            planned.add(("normed tokens read", b))
            tok = ring_t.free[k] = hi_lo(bank, t_hi[:, :], t_lo[:, :], t, free.get("t"))
            yield
            roped = []
            for j in range(2):
                i, bank, bfree = ring_a.take()
                roped.append(rope(j, bank, i, project(bank, w_hi, w_lo, j * D, tok, *folded[j], bfree)))
                yield
            i, bank, bfree = ring_a.take()
            free["t"] = done = project(bank, w_hi, w_lo, 2 * D, *folded[2], bfree)
            free["t busy"] = False
            must("values", b - 1)
            part = lambda n: vp[:, :, n * DH:(n + 1) * DH]
            vb = heads(bank)
            a = act.do(lambda e: e.activation(part(2), vb, ACT.Copy), done, free.get("vp"))
            a2 = ring_a.free[i] = dve.do(lambda e: e.tensor_tensor(heads(residue[:, :]), vb, part(2), ALU.subtract), a,
                                         free.get("residue"))
            a = act.do(lambda e: e.activation(part(1), heads(residue[:, :]), ACT.Copy), a2, free.get("vp"))
            free["residue"] = v_ready = pool.do(lambda e: e.tensor_tensor(
                part(0), heads(residue[:, :]), part(1), ALU.subtract), a, a2, free.get("vp"), other=dve,
                where=ENGINES["v low"])
            yield
            must("scores", b - 1)
            k, bank_q, bfree = ring_t.take()
            t = transpose4(bank_q, chunks(qk[:, 0, :]), roped[0], bfree)
            q_ready = ring_t.free[k] = act.do(lambda e: e.activation(qT[:, :], bank_q, ACT.Copy), t, free.get("qT"))
            yield
            k, bank_k, bfree = ring_t.take()
            t = transpose4(bank_k, chunks(qk[:, 1, :]), roped[1], bfree)
            free["qk"] = t
            k_ready = ()
            for h in range(4):
                rows = slice(h * DH, (h + 1) * DH)
                to, of = kbd[rows, :, h * T:(h + 1) * T], bank_k[rows, :].rearrange("p (g t) -> p g t", g=HG)
                k_ready += (act.do(lambda e, to=to, of=of: e.activation(to, of, ACT.Copy), t, free.get("kbd"), z_kbd,
                                   other=dve, other_make=lambda e, to=to, of=of: e.tensor_copy(to, of),
                                   where=KBD_ENGINE[h]),)
            ring_t.free[k] = k_ready
            free["qkv"] = q_ready, k_ready, v_ready
            planned.add(("projected", b))
            yield

        def self_attention(b):
            must("projected", b)
            x1 = x1s[:, b % X1, :]
            q_ready, k_ready, v_ready = free["qkv"]
            scale = DH ** -0.5

            def scores(g):
                i, bank, bfree = ring_a.take()
                e = mm(bank, qT[:, g * P:(g + 1) * P], kbd[:, g, :], True, True, q_ready, k_ready, bfree, signal=True,
                       n=4 * 512)
                free["qT"] = free["kbd"] = e
                j, _, sfree = ring_sc.take()
                s3 = sc[:, j, :].rearrange("p (h t) -> p h t", h=4)
                a = ring_a.free[i] = dve.do(lambda en: en.scalar_tensor_tensor(
                    s3, bank.rearrange("p (h t) -> p h t", h=4), scale,
                    mask[:, :].unsqueeze(1).to_broadcast([P, 4, T]), ALU.mult, ALU.add), e, consts, sfree)
                a = dve.do(lambda en: en.tensor_reduce(smax[:, j, :], s3, AX.X, ALU.max, negate=True), a, sfree)
                return j, tuple(act.do(lambda en, h=h: en.activation(
                    s3[:, h, :], s3[:, h, :], ACT.Exp, bias=smax[:, j, h:h + 1]), a, n=T + 190) for h in range(4))

            def probs_transposed(g, j, ready):
                k, bank, bfree = ring_t.take()
                t = transpose4(bank, chunks(sc[:, j, :]), ready, bfree)
                ring_sc.free[j] = t
                m, _, pfree = ring_pp.take()
                high, mid, low = (p_part[:, m, n, :] for n in range(3))
                a = act.do(lambda e: e.activation(high, bank, ACT.Copy), t, pfree,
                           other=dve, other_make=lambda e: e.tensor_copy(high, bank), where=ENGINES["p high"])
                r = ring_t.free[k] = dve.do(lambda e: e.tensor_tensor(residue[:, :], bank, high, ALU.subtract), a,
                                            free.get("residue"))
                a = act.do(lambda e: e.activation(mid, residue[:, :], ACT.Copy), r,
                           other=dve, other_make=lambda e: e.tensor_copy(mid, residue[:, :]), where=ENGINES["p middle"])
                free["residue"] = a = pool.do(lambda e: e.tensor_tensor(low, residue[:, :], mid, ALU.subtract), a, r,
                                              other=dve, where=LOW_ENGINE[g])
                return m, a

            def values(g, m, ready):
                i, bank, bfree = ring_a.take()
                for h in range(4):
                    for n in range(3):
                        e = mm(bank[:, h * VW + n * DH:(h + 1) * VW], p_part[:, m, n, h * T:(h + 1) * T],
                               vp[:, 4 * g + h, n * DH:VW], n == 0, n == 2, ready, v_ready, one_vp, bfree,
                               signal=h == 3 and n == 2, n=VW)
                ring_pp.free[m] = free["vp"] = e
                o4 = bank[:, 0:4 * VW].rearrange("p (h n) -> p h n", n=VW)
                y3 = heads(y[:, g * P:(g + 1) * P])
                r1 = dve.do(lambda en: en.reciprocal(sinv[:, :].unsqueeze(2), o4[:, :, 3 * DH:VW]), e, free.get("sinv"), n=8)
                r2 = ring_a.free[i] = dve.do(lambda en: en.tensor_reduce(
                    y3, o4[:, :, 0:3 * DH].rearrange("p h (i d) -> p h d i", i=3), AX.X, ALU.add), e, free.get("y"), follows=(r1,), n=384)
                free["sinv"] = r3 = dve.do(lambda en: en.tensor_tensor(
                    y3, y3, sinv[:, :].unsqueeze(2).to_broadcast([P, 4, DH]), ALU.mult), r1, r2, n=128, other=pool,
                    where=ENGINES["y"])
                return r3

            s_, p_ = {}, {}
            for what in B_STEPS:
                g = int(what[1])
                if what[0] == "s":
                    s_[g] = scores(g)
                elif what[0] == "p":
                    p_[g] = probs_transposed(g, *s_[g])
                else:
                    y_ready = values(g, *p_[g])
                planned.update({("scores", b)} if what == "s3" else {("values", b)} if what == "v3" else ())
                yield
            k, bank, bfree = ring_t.take()
            free["y"] = t = transpose4(bank, chunks(y), y_ready, bfree)
            assert not free.get("t busy"), "tokensT is still to be read"
            free["t busy"] = True
            tok = ring_t.free[k] = hi_lo(bank, t_hi[:, :], t_lo[:, :], t, free.get("t"))
            yield
            i, bank_c, bfree = ring_a.take()
            free["t"] = done = project(bank_c, wc_hi, wc_lo, 0, tok, *wc_split, bfree)
            free["t busy"] = False
            must("ffn", b - 1)
            x2 = ring_a.free[i] = dve.do(lambda e: e.tensor_tensor(x1, bank_c, x1, ALU.add), done)
            normed[b] = n = layernorm(2, x1, xn3[:, :], x2, free.get("xn3"))
            free["xn3r"] = residual[b] = dve.do(lambda e: e.tensor_tensor(x1, x1, xn3[:, :], ALU.add), n,
                                                  other=pool, where=ENGINES["x2 sum"])
            planned.add(("attended", b))
            yield

        normed, residual = {}, {}

        def ffn(b):
            x1 = x1s[:, b % X1, :]
            must("attended", b)
            k, bank_t3, bfree = ring_t.take()
            t = transpose4(bank_t3, chunks(xn3), normed[b], bfree)
            free["xn3"] = t
            tT = ring_t.free[k] = act.do(lambda e: e.activation(tT3[:, :], bank_t3, ACT.Copy), t, free.get("tT3"))
            yield
            i, bank_l, bfree = ring_a.take()
            reps = P // E
            for c in range(KD):
                e = mm(bank_l[:, 0:P], tT3[:, c * P:c * P + 1].to_broadcast([P, P]),
                       wr[:, c * E:(c + 1) * E].unsqueeze(1).to_broadcast([P, reps, E]), c == 0, c == KD - 1,
                       tT, bfree, signal=c == KD - 1)
            a = dve.do(lambda en: en.max(top[:, :], bank_l[:, 0:E]), e, free.get("gate"), n=8)
            a = ring_a.free[i] = picked = dve.do(
                lambda en: en.max_index(topi[:, :], top[:, :], bank_l[:, 0:E]), a, free.get("gate"), n=8)
            a = dve.do(lambda en: en.tensor_tensor(gt[:, 0:1], top[:, 1:2], top[:, 0:1], ALU.subtract), a,
                       free.get("gate"), n=1)
            a = act.do(lambda en: en.activation(gt[:, 1:2], gt[:, 0:1], ACT.Exp), a, n=1)
            a1 = dve.do(lambda en: en.tensor_scalar(gt[:, 2:3], gt[:, 1:2], 1.0, None, ALU.add), a, n=1)
            a1 = dve.do(lambda en: en.reciprocal(gt[:, 3:4], gt[:, 2:3]), a1, n=1)
            a2 = dve.do(lambda en: en.tensor_scalar(gt[:, 4:5], gt[:, 1:2], slot[:, 0:1], slot[:, 1:2],
                                                    ALU.mult, ALU.add), a, n=1)
            gate = dve.do(lambda en: en.tensor_tensor(gt[:, 5:6], gt[:, 4:5], gt[:, 3:4], ALU.mult), a1, a2, n=1)
            yield
            held = {}
            for n in range(2):
                def load_a(en, n=n):
                    held[n] = en.value_load(topi[0:1, n:n + 1], min_val=0, max_val=E - 1)
                    return en.dma_start(ya[:, :, n * R:(n + 1) * R],
                                        expA[bass.ds(held[n], 1), :, :].rearrange("o p (c r) -> (o p) c r", r=R))

                def load_b(en, n=n):
                    return en.dma_start(yb[n * R:(n + 1) * R, :],
                                        expB[bass.ds(held[n], 1), :, :].rearrange("o p n -> (o p) n"))
                expert_loads.load(sp, load_a, picked, free.get("experts"))
                experts = expert_loads.load(sp, load_b)
            yield
            i, bank_m, bfree = ring_a.take()
            for c in range(KD):
                e = mm(bank_m[:, 0:T], ya[:, c, :], tT3[:, c * P:(c + 1) * P], c == 0, c == KD - 1, experts, bfree,
                       signal=c == KD - 1)
            free["tT3"] = e
            m = ring_a.free[i] = dve.do(lambda en: en.tensor_scalar(midT[:, :], bank_m[:, 0:T], gt[:, 5:6],
                                                                    None, ALU.mult), e, gate, free.get("mid"), n=128)
            free["gate"] = m
            yield
            i, bank_f, bfree = ring_a.take()
            e = mm(bank_f, midT[:, :], yb[:, :], True, True, m, bfree, signal=True, n=4 * 512)
            free["experts"] = free["mid"] = e
            o = ring_a.free[i] = dve.do(lambda en: en.tensor_tensor(xn3[:, :], bank_f, x1, ALU.add), e,
                                        residual[b], free["xn3"])
            free[f"x1{b % X1}"] = o
            planned.add(("ffn", b))
            free["xn3"] = stores.load(sp, lambda en: en.dma_start(out[b], xn3[:, :]), o)
            yield

        def weights():
            for n in range(12):
                j, g = divmod(n, 4)
                r, cols = place["w", n] % RAW, slice(j * D + g * P, j * D + (g + 1) * P)
                k, bank, bfree = ring_a.take()
                for m in range(8):
                    c, half = divmod(m, 2)
                    at, shift = (m * 64, 0) if m < 7 else (384, 64)
                    e = mm(bank[:, at:at + P], raw[:, r, half * 512 + c * P:half * 512 + (c + 1) * P],
                           sc[:, 0, up_at[j] - shift:up_at[j] - shift + P], m < 7, m != 6,
                           arrived["w", n], consts, bfree, signal=m == 7, n=512)
                ring_a.free[k] = done = hi_lo(bank.rearrange("p (c n) -> p c n", c=KD), w_hi[:, :, cols],
                                              w_lo[:, :, cols], e)
                folded[j].append(done)
                used_piece(("w", n), e)
                yield
            ring_sc.free[0] = e
            for n in range(2):
                src = raw[:, place["w", 12 + n] % RAW, :].rearrange("p (k n) -> p k n", k=2)
                done = hi_lo(src, wc_hi[:, 2 * n:2 * n + 2, :], wc_lo[:, 2 * n:2 * n + 2, :], arrived["w", 12 + n],
                             n=PIECE)
                used_piece(("w", 12 + n), done)
                wc_split.append(done)
                planned.update({("weights", 0)} if n == 1 else ())
                yield

        folded, wc_split = [[], [], []], []
        send_pieces()
        for _ in prepare_query(0):
            pass

        streams = {
            "W": weights(),
            "X": chain.from_iterable(cross_attention(b) for b in range(NB)),
            "Q": chain.from_iterable(prepare_query(b) for b in range(1, NB)),
            "A": chain.from_iterable(projections(b) for b in range(NB)),
            "B": chain.from_iterable(self_attention(b) for b in range(NB)),
            "F": chain.from_iterable(ffn(b) for b in range(NB)),
        }
        work_of = {task: "setup" for task in program}
        for what in order_of_rounds():
            known = len(program)
            next(streams[what])
            work_of.update((task, what) for task in program[known:])
        assert all(next(stream, "end") == "end" for stream in streams.values())

        arrange(lanes, program, work_of)
        for lane in lanes:
            lane.number()

        with nc.Block() as block:
            @block.sync
            def _(eng):
                sp.play(eng)
                eng.wait_ge(stores.sem, stores.count)

            @block.tensor
            def _(eng):
                pe.play(eng)

            @block.scalar
            def _(eng):
                act.play(eng)

            @block.vector
            def _(eng):
                dve.play(eng)

            @block.gpsimd
            def _(eng):
                pool.play(eng)


def kernel(x, ctx_1024, L0_attn_Wq_down, L0_attn_Wk_down, L0_attn_Wv_down, L0_attn_Wq_up_c, L0_attn_Wq_up_e,
           L0_attn_Wk_up_c, L0_attn_Wk_up_e, L0_attn_Wv_up, L0_attn_Wc, L0_ffn_Wr, L0_ffn_A, L0_ffn_Bw):
    import concourse.bacc as bacc
    from concourse.bass_utils import run_bass_kernel_spmd

    a = np.asarray
    ctx = a(ctx_1024)
    ctxT = ctx.reshape(NB, NCH, 512, 2, 2, P).transpose(0, 1, 3, 5, 4, 2).reshape(NB, NPT, P, PIECE)
    ctxN = ctx.reshape(NB, NPT, 2, P, D).transpose(0, 1, 3, 2, 4).reshape(NB, NPT, P, PIECE)
    inv_freq = (1.0 / np.float32(10000.0) ** (np.arange(0, DHE, 2, dtype=np.float32) / np.float32(DHE))).astype(np.float32)
    angle = np.arange(T, dtype=np.float32)[:, None] * inv_freq[None, :]
    angle = np.concatenate((angle, angle), axis=-1)
    sign = np.where(np.arange(DHE) % 2 == 0, -1.0, 1.0).astype(np.float32)
    up = np.zeros((P, 512), np.float32)
    for head in range(2):
        for j, parts in enumerate(((L0_attn_Wq_up_c, L0_attn_Wq_up_e), (L0_attn_Wk_up_c, L0_attn_Wk_up_e),
                                   (L0_attn_Wv_up,))):
            col = 64 + 128 * j + head * DH
            up[head * L:(head + 1) * L, col:col + DH] = np.concatenate([a(p) for p in parts], axis=1)
    arrays = {
        "x": a(x), "ctxT": ctxT, "ctxN": ctxN,
        "wdT": np.stack([a(w).T.reshape(4, 2, P, D).transpose(0, 2, 1, 3).reshape(4, P, PIECE)
                         for w in (L0_attn_Wq_down, L0_attn_Wk_down, L0_attn_Wv_down)]),
"up": up,
        "wc": a(L0_attn_Wc).reshape(2, 2, P, D).transpose(0, 2, 1, 3).reshape(2, P, PIECE),
        "expA": a(L0_ffn_A).transpose(0, 2, 1).reshape(E, KD, P, R).transpose(0, 2, 1, 3).reshape(E, P, KD * R),
        "expB": a(L0_ffn_Bw).transpose(0, 2, 1),
        "const_t": np.concatenate((
            np.cos(angle), np.sin(angle) * sign,
            np.where(np.tril(np.ones((T, T), bool)), 0.0, MASK).astype(np.float32),
            np.stack([np.arange(P) >= R, np.arange(P) < R], axis=1).astype(np.float32),
            a(L0_ffn_Wr).T.reshape(KD, P, E).transpose(1, 0, 2).reshape(P, KD * E)), axis=1),
        "ident_t": np.eye(P, dtype=np.float32),
    }
    nc = bacc.Bacc("TRN2", target_bir_lowering=False, num_devices=1)
    arrays = {k: np.ascontiguousarray(v) for k, v in arrays.items()}
    args = [nc.dram_tensor(k, v.shape, mybir.dt.from_np(v.dtype), kind="ExternalInput").ap() for k, v in arrays.items()]
    out = nc.dram_tensor("out", (NB, T, D), F32, kind="ExternalOutput").ap()
    perceiver(nc, *args, out)
    return run_bass_kernel_spmd(nc, [arrays], core_ids=[0]).results[0]["out"]
```
